# Optimizing a Trainium2 kernel written in Bass

```python
import numpy as np
import jax
import jax.numpy as jnp

def _softmax(x, axis=-1):
    return jax.nn.softmax(x, axis=axis)

def _gelu(x):
    return jax.nn.gelu(x, approximate=True)

def _silu(x):
    return jax.nn.silu(x)

def _sigmoid(x):
    return jax.nn.sigmoid(x)

def _layernorm(x, axis=-1, eps=1e-05):
    m = jnp.mean(x, axis=axis, keepdims=True)
    v = jnp.var(x, axis=axis, keepdims=True)
    return (x - m) / jnp.sqrt(v + eps)

def _scatter_add(tgt, idx, src, axis=0):
    return tgt.at[idx].add(src)

def _segment_sum(src, seg, n):
    return jax.ops.segment_sum(src, seg, n)
kernel_name = 'mk_adj_ffn_d2_adj_r2_5d84c0'

def setup_inputs(seed: int=0):
    np.random.seed(seed)
    _w = jnp.asarray

    def _rec_inputs():
        import jax
        import jax.numpy as jnp
        _gk = jax.random.key(seed)
        x = 7.22e-05 + 1 * jax.random.normal(jax.random.fold_in(_gk, 1), (16, 512, 256), jnp.float32)
        _a = jax.random.bernoulli(jax.random.fold_in(_gk, 2), 0.00390625, (16, 512, 512))
        adj = _a.astype(jnp.int32)
        return (x, adj)
    x, adj = _rec_inputs()

    def _L0_gnn_setup():
        import jax, jax.numpy as jnp
        import numpy as np
        ALPHA = 0.2
        NEG_INF = -1000000000.0
        key = jax.random.key(seed)
        k1, k2, k3, k4, k5 = jax.random.split(key, 5)
        B, N, F_IN, F_OUT = (16, 512, 256, 256)
        graph_input = jax.random.normal(k1, (B, N, F_IN), dtype=jnp.float32)
        adj = jax.random.randint(k2, (B, N, N), 0, 2, dtype=jnp.int32)
        W = jax.random.normal(k3, (F_OUT, F_IN), dtype=jnp.float32) * (1.414 / np.sqrt(F_IN))
        a1 = jax.random.normal(k4, (F_OUT, 1), dtype=jnp.float32) * 0.1
        a2 = jax.random.normal(k5, (F_OUT, 1), dtype=jnp.float32) * 0.1
        return {'graph_input': graph_input, 'adj': adj, 'W': W, 'a1': a1, 'a2': a2}
    _L0_gnn_all = _L0_gnn_setup()
    _L0_gnn_in = {k: v for k, v in _L0_gnn_all.items() if k in ('W', 'a1', 'a2')}
    del _L0_gnn_all

    def _L0_ffn_setup():
        import jax, jax.numpy as jnp
        import numpy as np
        B, S, DIM, E, K = (8, 4096, 256, 4, 2)
        EPS = 1e-06
        key = jax.random.key(seed)
        ks = jax.random.split(key, 4)
        scale = 0.02
        return {'x': jax.random.normal(ks[0], (B, S, DIM), dtype=jnp.float32), 'router_w': jax.random.normal(ks[1], (DIM, E), dtype=jnp.float32) * scale, 'router_b': jnp.zeros((E,), jnp.float32), 'expert_w': jax.random.normal(ks[2], (E, DIM, DIM), dtype=jnp.float32) * scale, 'expert_b': jnp.zeros((E, DIM), jnp.float32), 'out_w': jax.random.normal(ks[3], (DIM, DIM), dtype=jnp.float32) * scale, 'out_b': jnp.zeros((DIM,), jnp.float32), 'norm_w': jnp.ones((DIM,), jnp.float32)}
    _L0_ffn_all = _L0_ffn_setup()
    _L0_ffn_in = {k: v for k, v in _L0_ffn_all.items() if k in ('router_w', 'router_b', 'expert_w', 'expert_b', 'out_w', 'out_b', 'norm_w')}
    del _L0_ffn_all

    def _L1_gnn_setup():
        import jax, jax.numpy as jnp
        import numpy as np
        ALPHA = 0.2
        K_NUM = 16
        NEG_INF = -9000000000000000.0
        key = jax.random.key(seed)
        k1, k2, k3, k4 = jax.random.split(key, 4)
        B, N, F_in, F_out = (4, 1024, 256, 256)
        h = jax.random.normal(k1, (B, N, F_in), dtype=jnp.float32)
        adj = jax.random.randint(k2, (B, N, N), 0, 2, dtype=jnp.int32)

        def xavier(k, shape, gain=1.414):
            fan_in, fan_out = (shape[0], shape[1])
            bound = gain * np.sqrt(6.0 / (fan_in + fan_out))
            return jax.random.uniform(k, shape, jnp.float32, -bound, bound)
        W = xavier(k3, (F_in, F_out))
        a = xavier(k4, (2 * F_out, 1))
        return {'h': h, 'adj': adj, 'W': W, 'a': a}
    _L1_gnn_all = _L1_gnn_setup()
    _L1_gnn_in = {k: v for k, v in _L1_gnn_all.items() if k in ('W', 'a')}
    del _L1_gnn_all

    def _L1_ffn_setup():
        import jax, jax.numpy as jnp
        import numpy as np
        TOP_K = 2
        key = jax.random.key(seed)
        ks = jax.random.split(key, 4)
        b, t, d, e, h = (2, 1024, 256, 8, 512)
        scale = 0.02
        return {'x': jax.random.normal(ks[0], (b, t, d), dtype=jnp.float32), 'router_w': jax.random.normal(ks[1], (e, d), dtype=jnp.float32) * scale, 'router_b': jnp.zeros((e,), dtype=jnp.float32), 'fc1_w': jax.random.normal(ks[2], (e, 2 * h, d), dtype=jnp.float32) * scale, 'fc1_b': jnp.zeros((e, 2 * h), dtype=jnp.float32), 'fc2_w': jax.random.normal(ks[3], (e, d, h), dtype=jnp.float32) * scale, 'fc2_b': jnp.zeros((e, d), dtype=jnp.float32)}
    _L1_ffn_all = _L1_ffn_setup()
    _L1_ffn_in = {k: v for k, v in _L1_ffn_all.items() if k in ('router_w', 'router_b', 'fc1_w', 'fc1_b', 'fc2_w', 'fc2_b')}
    del _L1_ffn_all
    return {'x': x, 'adj': adj, 'L0_gnn_W': _L0_gnn_in['W'], 'L0_gnn_a1': _L0_gnn_in['a1'], 'L0_gnn_a2': _L0_gnn_in['a2'], 'L0_ffn_router_w': _L0_ffn_in['router_w'], 'L0_ffn_router_b': _L0_ffn_in['router_b'], 'L0_ffn_expert_w': _L0_ffn_in['expert_w'], 'L0_ffn_expert_b': _L0_ffn_in['expert_b'], 'L0_ffn_out_w': _L0_ffn_in['out_w'], 'L0_ffn_out_b': _L0_ffn_in['out_b'], 'L0_ffn_norm_w': _L0_ffn_in['norm_w'], 'L1_gnn_W': _L1_gnn_in['W'], 'L1_gnn_a': _L1_gnn_in['a'], 'L1_ffn_router_w': _L1_ffn_in['router_w'], 'L1_ffn_router_b': _L1_ffn_in['router_b'], 'L1_ffn_fc1_w': _L1_ffn_in['fc1_w'], 'L1_ffn_fc1_b': _L1_ffn_in['fc1_b'], 'L1_ffn_fc2_w': _L1_ffn_in['fc2_w'], 'L1_ffn_fc2_b': _L1_ffn_in['fc2_b']}

def reference(x, adj, L0_gnn_W, L0_gnn_a1, L0_gnn_a2, L0_ffn_router_w, L0_ffn_router_b, L0_ffn_expert_w, L0_ffn_expert_b, L0_ffn_out_w, L0_ffn_out_b, L0_ffn_norm_w, L1_gnn_W, L1_gnn_a, L1_ffn_router_w, L1_ffn_router_b, L1_ffn_fc1_w, L1_ffn_fc1_b, L1_ffn_fc2_w, L1_ffn_fc2_b):
    import jax
    import jax.numpy as jnp

    def _L0_gnn_ref(graph_input, adj, W, a1, a2):
        import jax, jax.numpy as jnp
        import numpy as np
        ALPHA = 0.2
        NEG_INF = -1000000000.0
        h = jnp.einsum('bnf,of->bno', graph_input, W)
        f1 = h @ a1
        f2 = h @ a2
        e = f1 + jnp.swapaxes(f2, 1, 2)
        e = jax.nn.leaky_relu(e, negative_slope=ALPHA)
        scores = jnp.where(adj == 0, NEG_INF, e)
        attn = jax.nn.softmax(scores, axis=2)
        h_prime = jnp.einsum('bnm,bmf->bnf', attn, graph_input)
        return jax.nn.elu(h_prime)

    def _L0_ffn_ref(x, router_w, router_b, expert_w, expert_b, out_w, out_b, norm_w):
        import jax, jax.numpy as jnp
        import numpy as np
        B, S, DIM, E, K = (8, 4096, 256, 4, 2)
        EPS = 1e-06
        b, s, d = x.shape
        logits = x @ router_w + router_b
        topw, topi = jax.lax.top_k(logits, K)
        topw = jax.nn.softmax(topw, axis=-1)
        t = b * s
        xf = x.reshape(t, d)
        idx = topi.reshape(t, K)
        w = topw.reshape(t, K).astype(x.dtype)
        mask = jnp.zeros((t, E), x.dtype).at[jnp.arange(t)[:, None], idx].set(w)
        h = jax.nn.silu(jnp.einsum('td,edh->teh', xf, expert_w) + expert_b)
        comb = jnp.einsum('te,teh->th', mask, h)
        out = comb @ out_w + out_b
        y = xf + out
        rms = jnp.sqrt(jnp.mean(y * y, axis=-1, keepdims=True) + EPS)
        return (norm_w * (y / rms)).reshape(b, s, d)

    def _L1_gnn_ref(h, adj, W, a):
        import jax, jax.numpy as jnp
        import numpy as np
        ALPHA = 0.2
        K_NUM = 16
        NEG_INF = -9000000000000000.0
        F_out = W.shape[1]
        Wh = jnp.einsum('bnf,fo->bno', h, W)
        a1, a2 = (a[:F_out, 0], a[F_out:, 0])
        e_src = Wh @ a1
        e_dst = Wh @ a2
        e = e_src[:, :, None] + e_dst[:, None, :]
        e = jnp.where(e > 0, e, ALPHA * e)
        e = jnp.where(adj > 0, e, NEG_INF)
        attention = jax.nn.softmax(e, axis=2)
        topk_vals = jax.lax.top_k(attention, K_NUM)[0]
        kth = topk_vals[:, :, -1:]
        attention = jnp.where(attention < kth, 0.0, attention)
        h_prime = jnp.einsum('bij,bjo->bio', attention, Wh)
        return jax.nn.elu(h_prime)

    def _L1_ffn_ref(x, router_w, router_b, fc1_w, fc1_b, fc2_w, fc2_b):
        import jax, jax.numpy as jnp
        import numpy as np
        TOP_K = 2
        n_experts = router_w.shape[0]
        temp = 1.0
        logits = (jnp.einsum('btd,ed->bte', x, router_w) + router_b) / temp
        topk_val, topk_idx = jax.lax.top_k(logits, TOP_K)
        weights = jax.nn.softmax(topk_val, axis=-1)
        onehot = jax.nn.one_hot(topk_idx, n_experts, dtype=x.dtype)
        cw = jnp.einsum('btk,btke->bte', weights, onehot)
        h = jnp.einsum('btd,efd->btef', x, fc1_w) + fc1_b
        h1, h2 = jnp.split(h, 2, axis=-1)
        a = jax.nn.silu(h1) * h2
        y = jnp.einsum('bteh,edh->bted', a, fc2_w) + fc2_b
        out = jnp.einsum('bted,bte->btd', y, cw)
        return out
    x = x + _L0_gnn_ref(_layernorm(x, axis=-1), adj, L0_gnn_W, L0_gnn_a1, L0_gnn_a2)
    x = x + _L0_ffn_ref(_layernorm(x, axis=-1), L0_ffn_router_w, L0_ffn_router_b, L0_ffn_expert_w, L0_ffn_expert_b, L0_ffn_out_w, L0_ffn_out_b, L0_ffn_norm_w)
    x = x + _L1_gnn_ref(_layernorm(x, axis=-1), adj, L1_gnn_W, L1_gnn_a)
    x = x + _L1_ffn_ref(_layernorm(x, axis=-1), L1_ffn_router_w, L1_ffn_router_b, L1_ffn_fc1_w, L1_ffn_fc1_b, L1_ffn_fc2_w, L1_ffn_fc2_b)
    return x

_drawn_inputs = setup_inputs


def setup_inputs(seed=0):
    import zlib

    import numpy as np

    out = dict(_drawn_inputs(seed))
    spreads = {'L0_ffn_router_b': (0.0, 0.8),
     'L0_ffn_expert_b': (0.0, 0.8),
     'L0_ffn_out_b': (0.0, 0.1),
     'L0_ffn_norm_w': (1.0, 0.2),
     'L1_ffn_router_b': (0.0, 0.48),
     'L1_ffn_fc1_b': (0.0, 0.8),
     'L1_ffn_fc2_b': (0.0, 0.8)}
    factors = {'L0_ffn_router_w': 4.118,
     'L0_ffn_expert_w': 3.094,
     'L0_ffn_out_w': 2.852,
     'L1_ffn_fc1_w': 7.232,
     'L1_ffn_fc2_w': 7.202}
    for name, (base, spread) in spreads.items():
        noise = np.random.default_rng([zlib.crc32(name.encode()), seed]).standard_normal(out[name].shape)
        drawn = base * np.exp(spread * noise) if base else spread * noise
        out[name] = jnp.asarray(drawn.astype(out[name].dtype))
    for name, factor in factors.items():
        out[name] = (out[name] * factor).astype(out[name].dtype)
    return out
```

```python
import numpy as np
import concourse.bass as bass
from concourse import mybir
from contextlib import ExitStack

F32 = mybir.dt.float32
F16 = mybir.dt.float16
BF16 = mybir.dt.bfloat16
I32 = mybir.dt.int32
U32 = mybir.dt.uint32
ALU = mybir.AluOpType
ACT = mybir.ActivationFunctionType
AX = mybir.AxisListType

P = 128
B, N, D = 16, 512, 256
T = N // P
KC = D // P
H = T // 2
E0 = 4
E1 = 8
HID = 512
HC = HID // P
TOK = B * N
BANK = 512
U = 2
TURNS = B // U

SLOTS = 2 * P
REGION = TOK + SLOTS
ROW = D + E1 + 1
TILES = 2 * TOK // SLOTS + E1
TABLE = TILES + 3

SX = 16.0
SW = 64.0
SZ = SX * SW
NOT_LINKED = -2.0 ** 100
LN_EPS = 1e-05
RMS_EPS = 1e-06
SLOPE = 0.2

STAGES = ["gnn0", "ffn0", "gnn1", "route"]


def turn_plan():
    tr, mm, st = [], [], []
    for l in range(2):
        tr += [("xn", 2 * l, u, h) for u in range(U) for h in range(H)]
        if l:
            mm += [("wh", u, h) for u in range(U) for h in range(H)]
        st += [("p", l, u, t, k) for u in range(U) for t in range(T) for k in range(1 + l)]
        tr += [("p", l, u, t) for u in range(U) for t in range(T)]
        mm += [("attn", l, u, h) for u in range(U) for h in range(H)]
        if l == 0:
            tr += [("xn", 1, u, h) for u in range(U) for h in range(H)]
            mm += [("z", u, t, g) for u in range(U) for t in range(T) for g in range(2)]
            st += [("z", u, t, g) for u in range(U) for t in range(T) for g in range(2)]
            tr += [("comb", u, h) for u in range(U) for h in range(H)]
            mm += [("out", u, h) for u in range(U) for h in range(H)]
    tr += [("xn", 3, u, h) for u in range(U) for h in range(H)]
    return [{k: n for n, k in enumerate(x)} for x in (tr, mm, st)]


TR, MM, ST = turn_plan()
NTR, NMM, NST = 2, 4, 4
assert len(TR) % NTR == 0 and len(MM) % NMM == 0 and len(ST) % NST == 0


def build(nc, a, out):
    ctx = ExitStack()
    with ctx:
        def sb(name, shape, dt=F32):
            return ctx.enter_context(nc.sbuf_tensor(name, shape, dt))

        def sem(name):
            return ctx.enter_context(nc.semaphore(name))

        def sems(name, n):
            return [sem(f"{name}{k}") for k in range(n)]

        ident = sb("ident", [P, P])
        before = sb("before", [P, P], BF16)
        ones = sb("ones", [P, P], BF16)
        unscale = sb("unscale", [3, P], BF16)
        cst = sb("cst", [P, a["cst"].shape[1]])
        iota8, tok0, ebase, padtok = cst[:, 0:8], cst[:, 8:8 + T], cst[:, 12:20], cst[:, 20:22]
        jnum = cst[0:1, 22:22 + TABLE]
        nw = sb("nw", [P, D])
        rb0, rb1 = sb("rb0", [P, E0]), sb("rb1", [P, E1])
        rw1 = sb("rw1", [P, KC, E1])
        w0a, w1a = sb("w0a", [P, KC, 2]), sb("w1a", [P, KC, 2])
        u_src, u_dst = sb("u_src", [P, 2, KC, 1]), sb("u_dst", [P, 2, KC, P])
        gw1 = sb("gw1", [P, KC, D])
        ow = sb("ow", [P, KC, D])
        ewh, ewl = sb("ewh", [P, KC, E0 * D], F16), sb("ewl", [P, KC, E0 * D], F16)
        rwh, rwl = sb("rwh", [P, KC, E0], F16), sb("rwl", [P, KC, E0], F16)
        NB = E0 * D + D + E1 * D
        BSP = NB // P
        NB0 = E0 * D + D
        brow = sb("brow", [3, NB0], BF16)
        brow2 = ewh[0:3, :, :].rearrange("p k f -> p (k f)").bitcast(BF16)
        f1h, f1l = sb("f1h", [P, E1, KC, 2 * HID], F16), sb("f1l", [P, E1, KC, 2 * HID], F16)
        f2h, f2l = sb("f2h", [P, E1, HC, D], F16), sb("f2l", [P, E1, HC, D], F16)
        fb = sb("fb", [P, E1, 3 * HC])
        wst = sb("wst", [P, 2 * HID])

        adj = sb("adj", [P, T, N], I32)
        xin = [sb(f"xin{u}", [P, T, D]) for u in range(U)]
        xr = [sb(f"xr{u}", [P, T, D]) for u in range(U)]
        link = [sb(f"link{u}", [P, T, N], BF16) for u in range(U)]
        xn = [sb(f"xn{u}", [P, T, D]) for u in range(U)]
        xt = [sb(f"xt{u}", [P, KC, N]) for u in range(U)]
        S = [sb(f"S{u}", [P, T, N]) for u in range(U)]
        PT = [S[u][:, :, :].rearrange("p t (m n) -> p t m n", m=T) for u in range(U)]
        comb = [sb(f"comb{u}", [P, T, D]) for u in range(U)]
        pay = [sb(f"pay{u}", [P, T, ROW]) for u in range(U)]
        xh = [S[u][:, 0:2, :].rearrange("p a b -> p (a b)").bitcast(F16)
              .rearrange("p (s k n) -> p s k n", s=2, k=KC) for u in range(U)]
        stage = [sb(f"stage{k}", [P, BANK]) for k in range(NST)]
        SE = [S[u][:, :, :].rearrange("p (h two) n -> p h two n", two=2) for u in range(U)]

        stats, mv = sb("stats", [P, U, T, 6]), sb("mv", [P, U, T, 2])
        rstd, ve = sb("rstd", [P, U, T]), sb("ve", [P, U, T])
        mhalf = sb("mhalf", [P, T])
        src = sb("src", [P, U, T])
        mrow, mx, b1, b2 = (sb(n, [P, U, T]) for n in ("mrow", "mx", "b1", "b2"))
        top, top2 = sb("top", [P, U, T, 8]), sb("top2", [P, U, T, 8])
        rs, rinv = sb("rs", [P, U, T]), sb("rinv", [P, U, T])
        ss, rr = sb("ss", [P, U, T]), sb("rr", [P, U, T])
        lg, m8, i8 = sb("lg", [P, U, T, 8]), sb("m8", [P, U, T, 8]), sb("i8", [P, U, T, 8], U32)
        i8f = sb("i8f", [P, U, T, 2])
        dif, e2, den = sb("dif", [P, U, T]), sb("e2", [P, U, T]), sb("den", [P, U, T])
        w1, w2 = sb("w1", [P, U, T]), sb("w2", [P, U, T])
        oh1, oh2 = sb("oh1", [P, U, T, 8]), sb("oh2", [P, U, T, 8])
        g1, g2 = sb("g1", [P, U, T, 8]), sb("g2", [P, U, T, 8])
        gate0 = sb("gate0", [P, U, T, 8])
        chose = sb("chose", [P, U, T, 8], BF16)
        place = sb("place", [P, U, T, 8])
        slotf, slot = sb("slotf", [P, U, 2, T]), sb("slot", [P, U, 2, T], I32)
        base, tokf = sb("base", [P, E1]), sb("tokf", [P, U, T])
        pad = xin[0][:, :, :].rearrange("p t d -> p (t d)")[:, 0:2 * ROW].rearrange("p (s r) -> p s r", s=2)
        basei, cnti, tilesf, tcum = sb("basei", [1, E1], I32), sb("cnti", [1, E1], I32), sb("tilesf", [1, E1]), sb("tcum", [1, E1])
        zero8 = sb("zero8", [1, E1])
        tex, tst, tge = (xin[1][0:1, k, 0:TABLE] for k in range(3))
        tile_expert, tile_row = sb("tile_expert", [1, TABLE], I32), sb("tile_row", [1, TABLE], I32)
        gx = [pay[u][:, 0:2, :] for u in range(2)]
        gxh = [xt[u][:, 0, :].bitcast(F16).rearrange("p (s k n) -> p s k n", s=2, k=KC) for u in range(2)]
        ah = [xn[u][:, 0:2, :].rearrange("p a b -> p (a b)").bitcast(F16).rearrange("p (c n) -> p c n", c=HC) for u in range(2)]
        al = [xn[u][:, 2:4, :].rearrange("p a b -> p (a b)").bitcast(F16).rearrange("p (c n) -> p c n", c=HC) for u in range(2)]
        th = [S[0][:, c, 0:SLOTS] for c in range(HC)]
        z1 = [S[0][:, c, SLOTS:2 * SLOTS] for c in range(HC)]
        av = [S[1][:, c, 0:SLOTS] for c in range(HC)]
        ys = [comb[u][:, 0:2, :] for u in range(2)]
        gsel, tsel = sb("gsel", [P, 2, 2]), sb("tsel", [P, 2, 2], I32)
        bsel = sb("bsel", [P, 2, 3 * HC])

        def bank(name):
            return ctx.enter_context(nc.psum_tensor(name, [P, BANK], F32))
        ptr = [bank(f"ptr{k}") for k in range(NTR)]
        pmm = [bank(f"pmm{k}") for k in range(NMM)]
        pf = bank("pf")
        psm = bank("psm")
        SRC = [psm[:, 4 * u:4 * u + 4] for u in range(U)]
        LG0 = [psm[:, 16 + 16 * u:32 + 16 * u].rearrange("p (t e) -> p t e", t=T) for u in range(U)]
        LG1 = [psm[:, 64 + 32 * u:96 + 32 * u].rearrange("p (t e) -> p t e", t=T) for u in range(U)]
        POS = [psm[:, 128 + 32 * u:160 + 32 * u].rearrange("p (t e) -> p t e", t=T) for u in range(U)]
        TOT = [psm[:, 192 + 8 * u:200 + 8 * u] for u in range(U)]

        rows = nc.dram_tensor("rows", [E1 * REGION + SLOTS, ROW], F32, kind="Internal").ap()
        parts_d = nc.dram_tensor("parts_d", [3, NB], BF16, kind="Internal").ap()
        x_v = a["x"].rearrange("(b t p) d -> b p t d", p=P, t=T)
        adj_v = a["adj"].rearrange("(b t p) m -> b p t m", p=P, t=T)
        out_v = out[0:TOK, :].rearrange("(b t p) d -> b p t d", p=P, t=T)
        f1_v = a["f1"].rearrange("e (k p) f -> e p k f", p=P)
        f2_v = a["f2"].rearrange("e (k p) f -> e p k f", p=P)

        s_const = sem("consts_loaded")
        s_wld = sem("weights_loaded")
        s_bst, s_bl = sem("bias_rows_stored"), sem("bias_rows_loaded")
        s_setup = sem("setup_done")
        s_gs = sem("gpsimd_setup")
        s_up = sem("u_products")
        s_x = sems("x_loaded", U)
        s_adj = sem("adj_loaded")
        s_link = sem("link_ready")
        s_var = sem("variance_ready")
        s_rstd = sem("rstd_ready")
        s_xn = sem("xn_ready")
        s_trf = sem("transposed")
        s_mmf = sem("product_ready")
        s_relu = sem("attention_bank_read")
        s_zact = sem("expert_bank_read")
        s_xt = sem("xt_ready")
        s_xh = sem("xhi_ready")
        s_xl = sem("xlo_ready")
        s_f = sem("dst_scores_ready")
        s_srcp = sem("src_product")
        s_sc = sem("scores_ready")
        s_mxr = sem("max_ready")
        s_p = sem("exp_ready")
        s_keep = sem("kept_ready")
        s_pt = sem("pt_ready")
        s_wh = sem("wh_ready")
        s_elu = sem("elu_exp_ready")
        s_rinv = sem("rinv_ready")
        s_xr = sem("x_updated")
        s_lgp = sem("logits_ready")
        s_lgr = sem("logits_read")
        s_dif = sem("top2_gap_ready")
        s_e2 = sem("top2_exp_ready")
        s_tanh = sem("tanh_ready")
        s_stfree = sem("stage_used")
        s_y = sem("y_ready")
        s_ssq = sem("square_sum_ready")
        s_rr = sem("rms_ready")
        s_chose = sem("choice_ready")
        s_pos = sem("positions_ready")
        s_slot = sem("slots_ready")
        s_scat = sems("rows_scattered", U)
        s_store = sems("x_stored", U)
        s_wst = sem("expert_weights_loaded")
        s_wsp = sem("expert_weights_split")
        s_dve = sem("dve_step")
        s_pool = sem("pool_step")
        s_held = sem("held")
        s_table = sem("tile_table_ready")
        s_padw = sem("padding_written")
        s_gx = sems("rows_loaded", 2)
        s_gtr = sem("rows_transposed")
        s_gxh = sem("rows_hi_ready")
        s_gxl = sem("rows_lo_ready")
        s_bsel = sem("tile_biases_selected")
        s_sel = sem("tile_columns_selected")
        s_h = sem("hidden_ready")
        s_th = sem("hidden_act_ready")
        s_silu = sem("silu_ready")
        s_av = sem("gated_ready")
        s_ah = sem("gated_hi_ready")
        s_al = sem("gated_lo_ready")
        s_yp = sem("expert_out_ready")
        s_ys = sem("expert_out_scaled")
        s_add = sem("expert_out_added")

        def at(i, per, n):
            return i * per + n

        XN_PER, TR_PER, MM_PER, ST_PER = 4 * U * T, len(TR), len(MM), len(ST)
        XR_FIRST = 3 * U
        tr_keys, mm_keys, st_keys = list(TR), list(MM), list(ST)

        def tr_read(k):
            if k[0] == "p":
                return s_pt, 2 * U * T, (k[1] * U + k[2]) * T + k[3] + 1
            if k[:2] == ("xn", 1):
                return s_xl, U * H, k[2] * H + k[3] + 1
            use = 1 if k[0] == "comb" else k[1]
            return s_xt, 4 * U * H, (use * U + k[-2]) * H + k[-1] + 1

        def mm_read(k):
            if k[0] == "attn":
                return s_relu, 2 * U * H, (k[1] * U + k[2]) * H + k[3] + 1
            if k[0] == "z":
                return s_zact, 2 * U * T, (k[1] * T + k[2]) * 2 + k[3] + 1
            return (s_y if k[0] == "out" else s_wh), U * H, k[1] * H + k[2] + 1

        def st_read(k):
            if k[0] == "z":
                return s_stfree, 2 * U * T, (k[1] * T + k[2]) * 2 + k[3] + 1
            return s_keep, 2 * U * T, (k[1] * U + k[2]) * T + k[3] + 1

        def take(eng, i, plan, keys, key, ring, read):
            n = plan[key]
            if n >= ring:
                s, per, v = read(keys[n - ring])
                eng.wait_ge(s, at(i, per, v))
            return n % ring

        def hold(eng, s, v):
            eng.wait_ge(s, v)
            eng.sem_inc(s_held, 1)

        class Steps:

            def __init__(self, eng, s, per, i):
                self.eng, self.s, self.per, self.i, self.n = eng, s, per, i, 0

            def did(self, ins):
                ins.then_inc(self.s, 1)
                self.n += 1
                return self.n

            def wait(self, n=None):
                self.eng.wait_ge(self.s, self.base + at(self.i, self.per, self.n if n is None else n))

            def hold(self):
                hold(self.eng, self.s, self.base + at(self.i, self.per, self.n))

            base = 0

        block = ctx.enter_context(nc.Block())

        DVE_SETUP, DVE_TURN = a["dve_setup"], a["dve_turn"]
        POOL_SETUP, POOL_TURN = a["pool_setup"], a["pool_turn"]

        @block.sync
        def _(eng):
            eng.dma_start(ident[:, :], a["ident"]).then_inc(s_const, 16)
            eng.dma_start(xr[0][:, 2, 0:P], a["before"]).then_inc(s_const, 16)
            eng.dma_start(cst[:, :], a["cst"]).then_inc(s_const, 16)
            eng.dma_start(nw[:, :], a["nw"]).then_inc(s_const, 16)
            eng.dma_start(rw1[:, :, :], a["rw1"].rearrange("(k p) e -> p k e", p=P)).then_inc(s_const, 16)
            eng.dma_start(w0a[:, :, :], a["a0"].rearrange("(k p) e -> p k e", p=P)).then_inc(s_const, 16)
            eng.dma_start(w1a[:, :, :], a["a1"].rearrange("(k p) e -> p k e", p=P)).then_inc(s_const, 16)
            eng.dma_start(gw1[:, :, :], a["gw1"].rearrange("(k p) e -> p k e", p=P)).then_inc(s_const, 16)
            eng.dma_start(ow[:, :, :], a["ow"].rearrange("(k p) e -> p k e", p=P)).then_inc(s_const, 16)
            eng.dma_start(S[1][:, :, :].rearrange("p (k a) n -> p k (a n)", k=KC), a["ew"].rearrange("(k p) f -> p k f", p=P)).then_inc(s_wld, 16)
            eng.dma_start(xr[0][:, 1, 0:KC * E0].rearrange("p (k e) -> p k e", k=KC), a["rw0"].rearrange("(k p) e -> p k e", p=P)).then_inc(s_wld, 16)
            eng.dma_start(S[0][:, 0, :].rearrange("p (k f) -> p k f", k=KC), a["gw0t"].rearrange("(k p) e -> p k e", p=P)).then_inc(s_wld, 16)
            eng.dma_start(S[0][:, 1, :].rearrange("p (k f) -> p k f", k=KC), a["gw1t"].rearrange("(k p) e -> p k e", p=P)).then_inc(s_wld, 16)
            eng.dma_start(xr[0][:, 0, 0:E1 * 2 * HC], a["fb1"]).then_inc(s_wld, 16)
            eng.dma_start(xr[1][:, 0, 0:BSP], a["brow"]).then_inc(s_wld, 16)
            eng.wait_ge(s_setup, 1)
            for k in range(3):
                eng.dma_start(parts_d[k, :].rearrange("(p b) -> p b", p=P), xn[0][:, k, 0:BSP // 2].bitcast(BF16)[:, 0:BSP]).then_inc(s_bst, 16)
            eng.wait_ge(s_bst, 48)
            eng.dma_start(brow[:, :], parts_d[:, 0:NB0]).then_inc(s_bl, 16)
            eng.wait_ge(s_setup, 2)
            with eng.Fori(0, TURNS) as i:
                for u in range(U):
                    hold(eng, s_xr, at(i, 3 * U, u + 1))
                    eng.dma_start(xin[u][:, :, :], x_v[bass.ds(i * U + u, 1)].rearrange("b p t d -> p (b t) d")).then_inc(s_x[u], 16)
                    hold(eng, s_link, at(i, U, u + 1))
                    eng.dma_start(adj[:, :, :], adj_v[bass.ds(i * U + u, 1)].rearrange("b p t d -> p (b t) d")).then_inc(s_adj, 16)
                for k in range(KC):
                    hold(eng, s_wsp, at(i, 3, k + 1))
                    eng.dma_start(wst[:, :], f1_v[bass.ds(i, 1), :, k, :].rearrange("e p f -> p (e f)")).then_inc(s_wst, 16)
                hold(eng, s_wsp, at(i, 3, 3))
                eng.dma_start(wst[:, :].rearrange("p (k f) -> p k f", k=HC), f2_v[bass.ds(i, 1)].rearrange("e p k f -> p (e k) f")).then_inc(s_wst, 16)
            for u in range(U):
                eng.wait_ge(s_scat[u], 16 + TURNS * 2 * T * 16)
                eng.wait_ge(s_store[u], 16 + TURNS * 16)
            eng.wait_ge(s_table, 1)
            for e in range(E1):
                r = eng.value_load(basei[0:1, e:e + 1], min_val=0, max_val=E1 * REGION)
                eng.dma_start(rows[bass.ds(r, SLOTS), :].rearrange("(s p) d -> p s d", p=P), pad).then_inc(s_padw, 16)
            eng.wait_ge(s_padw, 16 * E1)
            eng.wait_ge(s_add, 48)
            for j in range(2):
                r = eng.value_load(tile_row[0:1, j + 1:j + 2], min_val=0, max_val=E1 * REGION)
                eng.dma_start(gx[j], rows[bass.ds(r, SLOTS), :].rearrange("(s p) d -> p s d", p=P)).then_inc(s_gx[j], 16)
            with eng.Fori(0, TILES // 2) as i:
                for v in range(2):
                    hold(eng, s_sel, at(i, 2, v + 2))
                    hold(eng, s_gtr, at(i, 2, v + 1))
                    r = eng.value_load(tile_row[0:1, bass.ds(i * 2 + v + 3, 1)], min_val=0, max_val=E1 * REGION)
                    eng.dma_start(gx[v], rows[bass.ds(r, SLOTS), :].rearrange("(s p) d -> p s d", p=P)).then_inc(s_gx[v], 16)
            for v in range(2):
                eng.wait_ge(s_gx[v], 16 * (TILES // 2 + 1))
            eng.wait_ge(s_add, 48 + TILES * 2 * 16)

        @block.gpsimd
        def _(eng):
            for s, n in ([(s_xr, XR_FIRST), (s_link, 1), (s_wsp, 1), (s_av, HC), (s_sel, 1)]
                         + [(s, 16) for s in s_store]):
                eng.sem_inc(s, n)
            eng.dma_start(rb0[:, :], a["rb0"]).then_inc(s_scat[0], 16)
            eng.dma_start(rb1[:, :], a["rb1"]).then_inc(s_scat[1], 16)
            st = Steps(eng, s_pool, POOL_TURN, 0)
            eng.memset(mhalf[:, :], -0.5).then_inc(s_gs, 1)
            eng.memset(ones[:, :], 1.0).then_inc(s_gs, 1)
            eng.memset(unscale[:, :], 1.0 / SZ).then_inc(s_gs, 1)
            eng.wait_ge(s_gs, 3)
            with eng.Fori(0, TURNS) as i:
                st = Steps(eng, s_pool, POOL_TURN, i)

                def rsqrt(o, v, scale, eps, ready):
                    u = ve[:, ready[2], :]
                    st.did(eng.tensor_scalar(u, v, scale, eps, ALU.mult, ALU.add))
                    st.wait()
                    eng.tensor_tensor(o, u, mhalf[:, :], ALU.pow).then_inc(ready[0], 1)

                def norm(j):
                    for u in range(U):
                        hold(eng, s_var, at(i, 4 * U, j * U + u + 1))
                        rsqrt(rstd[:, u, :], mv[:, u, :, 1], 1.0, LN_EPS, (s_rstd, None, u))

                norm(0)
                for u in range(U):
                    hold(eng, s_adj, at(i, 16 * U, 16 * (u + 1)))
                    eng.tensor_scalar(link[u][:, :, :], adj[:, :, :], -NOT_LINKED, NOT_LINKED, ALU.mult, ALU.add).then_inc(s_link, 1)
                norm(1)

                def split(n, hi, lo):
                    w = wst[:, :]
                    hold(eng, s_wst, at(i, 48, 16 * (n + 1)))
                    st.did(eng.tensor_scalar(w, w, SW, 0.0, ALU.mult, ALU.add))
                    st.wait()
                    st.did(eng.tensor_copy(hi, w))
                    st.wait()
                    eng.tensor_tensor(lo, w, hi, ALU.subtract).then_inc(s_wsp, 1)

                split(0, *(w[:, bass.ds(i, 1), 0, :].rearrange("p e f -> p (e f)") for w in (f1h, f1l)))
                for u in range(U):
                    hold(eng, s_ssq, at(i, U * T, (u + 1) * T))
                    rsqrt(rr[:, u, :], ss[:, u, :], 1.0 / D, RMS_EPS, (s_rr, None, u))
                split(1, *(w[:, bass.ds(i, 1), 1, :].rearrange("p e f -> p (e f)") for w in (f1h, f1l)))
                norm(2)
                split(2, *(w[:, bass.ds(i, 1), :, :].rearrange("p e k f -> p (e k f)") for w in (f2h, f2l)))
                norm(3)
                for u in range(U):
                    hold(eng, s_slot, at(i, U, u + 1))
                    for k in range(2):
                        for t in range(T):
                            eng.indirect_dma_start(rows, bass.IndirectOffsetOnAxis(slot[:, u, k, t:t + 1], 0),
                                                   pay[u][:, t, :], None).then_inc(s_scat[u], 16)
                assert st.n == POOL_TURN, st.n
            eng.wait_ge(s_table, 1)
            eng.dma_start(out[TOK:TOK + SLOTS, :].rearrange("(s p) d -> p s d", p=P), pad[:, :, 0:D]).then_inc(s_add, 16)
            eng.dma_start(rows[E1 * REGION:, :].rearrange("(s p) d -> p s d", p=P), pad).then_inc(s_add, 16)
            eng.dma_start(brow2, parts_d[:, NB0:NB]).then_inc(s_add, 16)
            with eng.Fori(0, TILES // 2) as i:
                for v in range(2):
                    hold(eng, s_ys, at(i, 2, v + 1))
                    hold(eng, s_add, at(i, 64, 48 + 32 * v))
                    q = 1 - v
                    for s in range(2):
                        eng.indirect_dma_start(out, bass.IndirectOffsetOnAxis(tsel[:, q, s:s + 1], 0),
                                               ys[q][:, s, :], None, compute_op=ALU.add).then_inc(s_add, 16)

        @block.scalar
        def _(eng):
            def per_turn(i):
                def tr_wait(k):
                    eng.wait_ge(s_trf, at(i, TR_PER, TR[k] + 1))

                def xt_copy(j):
                    for u in range(U):
                        for h in range(H):
                            k = ("xn", j, u, h)
                            tr_wait(k)
                            eng.activation(xt[u][:, :, h * 2 * P:(h + 1) * 2 * P],
                                           ptr[TR[k] % NTR][:, :].rearrange("p (k n) -> p k n", k=KC), ACT.Copy)\
                               .then_inc(s_xt, 1)

                def gnn(l):
                    xt_copy(2 * l)
                    for u in range(U):
                        if l:
                            for h in range(H):
                                k = MM[("wh", u, h)]
                                eng.wait_ge(s_mmf, at(i, MM_PER, k + 1))
                                eng.activation(comb[u][:, 2 * h:2 * h + 2, :].rearrange("p t d -> p (t d)"), pmm[k % NMM][:, :],
                                               ACT.Copy).then_inc(s_wh, 1)
                        eng.wait_ge(s_mxr, at(i, 2 * U, l * U + u + 1))
                        for t in range(T):
                            o1 = stage[take(eng, i, ST, st_keys, ("p", l, u, t, 0), NST, st_read)][:, :]
                            eng.activation(o1, S[u][:, t, :], ACT.Exp, bias=b1[:, u, t:t + 1]).then_inc(s_p, 1)
                            o2 = stage[take(eng, i, ST, st_keys, ("p", l, u, t, 1), NST, st_read)][:, :] if l else S[u][:, t, :]
                            eng.activation(o2, S[u][:, t, :], ACT.Exp, bias=b2[:, u, t:t + 1], scale=SLOPE).then_inc(s_p, 1)
                    for u in range(U):
                        for t in range(T):
                            k = ("p", l, u, t)
                            tr_wait(k)
                            eng.activation(PT[u][:, t, :, :], ptr[TR[k] % NTR][:, :].rearrange("p (k n) -> p k n", k=T),
                                           ACT.Copy).then_inc(s_pt, 1)
                    for u in range(U):
                        eng.wait_ge(s_rinv, at(i, 2 * U, l * U + u + 1))
                        for h in range(H):
                            k = MM[("attn", l, u, h)]
                            eng.wait_ge(s_mmf, at(i, MM_PER, k + 1))
                            for t2 in range(2):
                                t = 2 * h + t2
                                eng.activation(SE[u][:, h, 0, t2 * D:(t2 + 1) * D], pmm[k % NMM][:, t2 * D:(t2 + 1) * D],
                                               ACT.Exp, scale=rinv[:, u, t:t + 1]).then_inc(s_elu, 1)

                gnn(0)
                for u in range(U):
                    for h in range(H):
                        k = ("xn", 1, u, h)
                        tr_wait(k)
                        eng.activation(xh[u][:, 0, :, h * 2 * P:(h + 1) * 2 * P],
                                       ptr[TR[k] % NTR][:, :].rearrange("p (k n) -> p k n", k=KC), ACT.Copy, scale=SX)\
                           .then_inc(s_xh, 1)
                for u in range(U):
                    for t in range(T):
                        for g in range(2):
                            k = MM[("z", u, t, g)]
                            eng.wait_ge(s_mmf, at(i, MM_PER, k + 1))
                            q = take(eng, i, ST, st_keys, ("z", u, t, g), NST, st_read)
                            eng.activation(stage[q][:, :], pmm[k % NMM][:, :], ACT.Tanh, scale=0.5 / SZ).then_inc(s_tanh, 1)
                        if t == 0:
                            eng.wait_ge(s_dif, at(i, 2 * U, u + 1))
                            eng.activation(e2[:, u, :], dif[:, u, :], ACT.Exp).then_inc(s_e2, 1)
                for u in range(U):
                    for h in range(H):
                        k = ("comb", u, h)
                        tr_wait(k)
                        eng.activation(xt[u][:, :, h * 2 * P:(h + 1) * 2 * P],
                                       ptr[TR[k] % NTR][:, :].rearrange("p (k n) -> p k n", k=KC), ACT.Copy)\
                           .then_inc(s_xt, 1)
                for u in range(U):
                    for h in range(H):
                        eng.wait_ge(s_y, at(i, U * H, u * H + h + 1))
                        for t in (2 * h, 2 * h + 1):
                            eng.activation(S[u][:, t, 0:D], comb[u][:, t, :], ACT.Square, accum_out=ss[:, u, t:t + 1]).then_inc(s_ssq, 1)
                gnn(1)
                xt_copy(3)
                for u in range(U):
                    eng.wait_ge(s_dif, at(i, 2 * U, U + u + 1))
                    eng.activation(e2[:, u, :], dif[:, u, :], ACT.Exp).then_inc(s_e2, 1)
                    eng.wait_ge(s_xr, at(i, 3 * U, 3 * U + 2 * U + u + 1))
                    eng.dma_start(out_v[bass.ds(i * U + u, 1)].rearrange("b p t d -> p (b t) d"), xr[u][:, :, :]).then_inc(s_store[u], 16)

            with eng.Fori(0, TURNS) as i:
                per_turn(i)

            eng.wait_ge(s_gtr, 1)
            eng.activation(gxh[0][:, 0, :, :], ptr[0][:, :].rearrange("p (k n) -> p k n", k=KC), ACT.Copy, scale=SX).then_inc(s_gxh, 1)
            with eng.Fori(0, TILES // 2) as i:
                for v in range(2):
                    q = 1 - v
                    eng.wait_ge(s_bsel, at(i, 2, v + 1))
                    for c in range(HC):
                        eng.wait_ge(s_h, at(i, 2 * HC, v * HC + c + 1))
                        eng.activation(th[c], pmm[c][:, 0:SLOTS], ACT.Tanh, scale=0.5 / SZ, bias=bsel[:, v, c:c + 1]).then_inc(s_th, 1)
                        eng.activation(z1[c], pmm[c][:, 0:SLOTS], ACT.Identity, scale=0.5 / SZ * SX / SZ,
                                       bias=bsel[:, v, HC + c:HC + c + 1]).then_inc(s_th, 1)
                        if c >= 1:
                            eng.wait_ge(s_av, at(i, 2 * HC, HC + v * HC + c))
                            eng.activation(ah[v][:, c - 1, :], av[c - 1], ACT.Copy).then_inc(s_ah, 1)
                    eng.wait_ge(s_gtr, at(i, 2, v + 2))
                    eng.activation(gxh[q][:, 0, :, :], ptr[q][:, :].rearrange("p (k n) -> p k n", k=KC), ACT.Copy, scale=SX).then_inc(s_gxh, 1)
                    eng.wait_ge(s_av, at(i, 2 * HC, HC + v * HC + HC))
                    eng.activation(ah[v][:, HC - 1, :], av[HC - 1], ACT.Copy).then_inc(s_ah, 1)
                    eng.wait_ge(s_yp, at(i, 2, v + 1))
                    eng.wait_ge(s_add, at(i, 64, 16 + 32 * v))
                    eng.wait_ge(s_sel, at(i, 2, v + 1))
                    for s in range(2):
                        ins = eng.activation(ys[q][:, s, :], (pf if q else psm)[:, s * D:(s + 1) * D], ACT.Copy, scale=gsel[:, q, s:s + 1])
                    ins.then_inc(s_ys, 1)

        @block.tensor
        def _(eng):
            eng.wait_ge(s_const, 16 * 9)
            eng.wait_ge(s_wld, 16 * 6)
            for l, wa in ((0, w0a), (1, w1a)):
                for m in range(KC):
                    for k in range(KC):
                        ins = eng.matmul(psm[:, 4 * l + 2 * m:4 * l + 2 * m + 2],
                                         S[0][:, l, k * D + m * P:k * D + (m + 1) * P], wa[:, k, :],
                                         start=(k == 0), stop=(k == KC - 1))
            ins.then_inc(s_up, 1)
            eng.wait_ge(s_setup, 2)
            eng.wait_ge(s_bl, 16)
            eng.wait_ge(s_gs, 3)

            with eng.Fori(0, TURNS) as i:
                def tr_take(k):
                    return ptr[take(eng, i, TR, tr_keys, k, NTR, tr_read)]

                def mm_take(k):
                    return pmm[take(eng, i, MM, mm_keys, k, NMM, mm_read)]

                def turn_rows(k, u, h, x):
                    o = tr_take(k)
                    for c in range(KC):
                        for t2 in range(2):
                            ins = eng.transpose(o[:, c * 2 * P + t2 * P:c * 2 * P + (t2 + 1) * P],
                                                x[:, 2 * h + t2, c * P:(c + 1) * P], ident[:, :])
                    ins.then_inc(s_trf, 1)

                def turn_xn(j):
                    for u in range(U):
                        for h in range(H):
                            eng.wait_ge(s_xn, at(i, XN_PER, (j * U + u) * T + 2 * h + 2))
                            turn_rows(("xn", j, u, h), u, h, pay[u] if j == 3 else xn[u])

                def xt_at(use, u):
                    eng.wait_ge(s_xt, at(i, 4 * U * H, (use * U + u + 1) * H))

                def gnn(l):
                    turn_xn(2 * l)
                    for u in range(U):
                        xt_at(2 * l, u)
                        if l or u:
                            eng.wait_ge(s_sc, at(i, 2 * U * T, (l * U + u) * T))
                        for t in range(T):
                            for c in range(KC):
                                ins = eng.matmul(SRC[u][:, t:t + 1], xt[u][:, c, t * P:(t + 1) * P], u_src[:, l, c, :],
                                                 start=(c == 0), stop=(c == KC - 1))
                        ins.then_inc(s_srcp, 1)
                        for c in range(KC):
                            ins = eng.matmul(pf[:, :], u_dst[:, l, c, :], xt[u][:, c, :], start=(c == 0), stop=(c == KC - 1))
                        ins.then_inc(s_f, 1)
                        if l:
                            for h in range(H):
                                o = mm_take(("wh", u, h))
                                for t2 in range(2):
                                    t = 2 * h + t2
                                    for c in range(KC):
                                        ins = eng.matmul(o[:, t2 * D:(t2 + 1) * D], xt[u][:, c, t * P:(t + 1) * P], gw1[:, c, :],
                                                         start=(c == 0), stop=(c == KC - 1))
                                ins.then_inc(s_mmf, 1)
                    for u in range(U):
                        for t in range(T):
                            k = ("p", l, u, t)
                            eng.wait_ge(s_keep, at(i, 2 * U * T, (l * U + u) * T + t + 1))
                            o = tr_take(k)
                            for m in range(T):
                                ins = eng.transpose(o[:, m * P:(m + 1) * P], S[u][:, t, m * P:(m + 1) * P], ident[:, :])
                            ins.then_inc(s_trf, 1)
                    for u in range(U):
                        if l:
                            eng.wait_ge(s_wh, at(i, U * H, (u + 1) * H))
                        val = comb[u] if l else xn[u]
                        for h in range(H):
                            eng.wait_ge(s_pt, at(i, 2 * U * T, (l * U + u) * T + 2 * h + 2))
                            o = mm_take(("attn", l, u, h))
                            for t2 in range(2):
                                for m in range(T):
                                    ins = eng.matmul(o[:, t2 * D:(t2 + 1) * D], PT[u][:, 2 * h + t2, m, :], val[:, m, :],
                                                     start=(m == 0), stop=(m == T - 1))
                            ins.then_inc(s_mmf, 1)

                gnn(0)
                turn_xn(1)
                for u in range(U):
                    eng.wait_ge(s_xl, at(i, U * H, (u + 1) * H))
                    if u:
                        eng.wait_ge(s_lgr, at(i, 2 * U, u))
                    for t in range(T):
                        n = 0
                        for c in range(KC):
                            for s, w in ((0, rwh), (1, rwh), (0, rwl)):
                                ins = eng.matmul(LG0[u][:, t, :], xh[u][:, s, c, t * P:(t + 1) * P], w[:, c, :],
                                                 start=(n == 0), stop=(n == 5))
                                n += 1
                    ins.then_inc(s_lgp, 1)
                    for t in range(T):
                        for g in range(2):
                            o = mm_take(("z", u, t, g))
                            eng.matmul(o[:, :], ones[0:3, :], brow[:, g * BANK:(g + 1) * BANK], start=True, stop=False)
                            for c in range(KC):
                                for s, w in ((0, ewh), (0, ewl), (1, ewh)):
                                    ins = eng.matmul(o[:, :], xh[u][:, s, c, t * P:(t + 1) * P], w[:, c, g * BANK:(g + 1) * BANK],
                                                     start=False, stop=(c == KC - 1 and s == 1))
                            ins.then_inc(s_mmf, 1)
                for u in range(U):
                    for h in range(H):
                        eng.wait_ge(s_stfree, at(i, 2 * U * T, (u * T + 2 * h + 2) * 2))
                        turn_rows(("comb", u, h), u, h, comb[u])
                for u in range(U):
                    xt_at(1, u)
                    for h in range(H):
                        o = mm_take(("out", u, h))
                        for t2 in range(2):
                            t = 2 * h + t2
                            eng.matmul(o[:, t2 * D:(t2 + 1) * D], unscale[:, :], brow[:, E0 * D:E0 * D + D], start=True, stop=False)
                            for c in range(KC):
                                ins = eng.matmul(o[:, t2 * D:(t2 + 1) * D], xt[u][:, c, t * P:(t + 1) * P], ow[:, c, :],
                                                 start=False, stop=(c == KC - 1))
                        ins.then_inc(s_mmf, 1)
                gnn(1)
                turn_xn(3)
                for u in range(U):
                    xt_at(3, u)
                    if u:
                        eng.wait_ge(s_lgr, at(i, 2 * U, U + u))
                    for t in range(T):
                        for c in range(KC):
                            ins = eng.matmul(LG1[u][:, t, :], xt[u][:, c, t * P:(t + 1) * P], rw1[:, c, :],
                                             start=(c == 0), stop=(c == KC - 1))
                    ins.then_inc(s_lgp, 1)
                for u in range(U):
                    eng.wait_ge(s_chose, at(i, U, u + 1))
                    eng.wait_ge(s_lgr, at(i, 2 * U, 2 * U))
                    for t in range(T):
                        for t1 in range(t + 1):
                            eng.matmul(POS[u][:, t, :], before[:, :] if t1 == t else ones[:, :], chose[:, u, t1, :],
                                       start=(t1 == 0), stop=(t1 == t))
                    for t in range(T):
                        ins = eng.matmul(TOT[u], ones[:, :], chose[:, u, t, :], start=(t == 0), stop=(t == T - 1))
                    ins.then_inc(s_pos, 1)

            def turn_tile(v):
                for c in range(KC):
                    for s in range(2):
                        ins = eng.transpose(ptr[v][:, c * SLOTS + s * P:c * SLOTS + (s + 1) * P],
                                            gx[v][:, s, c * P:(c + 1) * P], ident[:, :])
                ins.then_inc(s_gtr, 1)

            eng.wait_ge(s_gx[0], 16)
            turn_tile(0)
            eng.wait_ge(s_wsp, 1 + 3 * TURNS)
            eng.wait_ge(s_add, 48)
            eng.wait_ge(s_table, 2)
            with eng.Fori(0, TILES // 2) as i:
                for v in range(2):
                    q = 1 - v
                    e = eng.value_load(tile_expert[0:1, bass.ds(i * 2 + v + 1, 1)], min_val=0, max_val=E1 - 1)
                    eng.wait_ge(s_gxl, at(i, 2, v + 1))
                    for c in range(HC):
                        eng.wait_ge(s_av, at(i, 2 * HC, v * HC + c + 1))
                        for half in range(2):
                            n = 0
                            for k in range(KC):
                                f = half * HID + c * P
                                for w, s in ((f1h, 0), (f1h, 1), (f1l, 0)):
                                    ins = eng.matmul(pmm[c][:, half * SLOTS:(half + 1) * SLOTS],
                                                     w[:, bass.ds(e, 1), k, f:f + P].rearrange("p e f -> p (e f)"),
                                                     gxh[v][:, s, k, :], start=(n == 0), stop=(n == 5))
                                    n += 1
                        ins.then_inc(s_h, 1)
                    eng.wait_ge(s_gx[q], at(i, 16, 16 + 16 * v))
                    turn_tile(q)
                    hold(eng, s_al, at(i, 2 * HC, v * HC + 1))
                    e = eng.value_load(tile_expert[0:1, bass.ds(i * 2 + v, 1)], min_val=0, max_val=E1 - 1)
                    y = pf if q else psm
                    for s in range(2):
                        o = y[:, s * D:(s + 1) * D]
                        eng.matmul(o, ones[0:3, :], brow2[:, bass.ds(e * D, D)], start=True, stop=False)
                        for c in range(HC):
                            for x, w in ((ah, f2h), (ah, f2l), (al, f2h)):
                                ins = eng.matmul(o, x[q][:, c, s * P:(s + 1) * P],
                                                 w[:, bass.ds(e, 1), c, :].rearrange("p e f -> p (e f)"),
                                                 start=False, stop=(c == HC - 1 and x is al))
                    ins.then_inc(s_yp, 1)

        @block.vector
        def _(eng):
            st = Steps(eng, s_dve, 0, 0)
            did, wait = st.did, st.wait
            eng.wait_ge(s_wld, 16 * 6)
            eng.wait_ge(s_const, 16 * 9)
            b, r1, r2 = (xr[1][:, k, 0:BSP] for k in range(3))
            parts = [xn[0][:, k, 0:BSP // 2].bitcast(BF16)[:, 0:BSP] for k in range(3)]
            did(eng.tensor_scalar(b, b, SZ, 0.0, ALU.mult, ALU.add))
            wait()
            did(eng.tensor_copy(parts[0], b))
            wait()
            did(eng.tensor_tensor(r1, b, parts[0], ALU.subtract))
            wait()
            did(eng.tensor_copy(parts[1], r1))
            wait()
            did(eng.tensor_tensor(r2, r1, parts[1], ALU.subtract))
            wait()
            eng.tensor_copy(parts[2], r2).then_inc(s_setup, 1)
            did(eng.tensor_copy(before[:, :], xr[0][:, 2, 0:P]))
            did(eng.memset(lg[:, :, :, :], NOT_LINKED))
            did(eng.tensor_copy(base[:, :], ebase))
            did(eng.tensor_copy(tokf[:, 0, :], tok0))
            did(eng.tensor_scalar(tokf[:, 1, :], tok0, float(N), 0.0, ALU.add, ALU.add))
            for w, hi, lo in ((S[1][:, :, :].rearrange("p a n -> p (a n)"), ewh[:, :, :].rearrange("p k f -> p (k f)"), ewl[:, :, :].rearrange("p k f -> p (k f)")),
                              (xr[0][:, 1, 0:KC * E0], rwh[:, :, :].rearrange("p k f -> p (k f)"), rwl[:, :, :].rearrange("p k f -> p (k f)"))):
                did(eng.tensor_scalar(hi, w, SW, 0.0, ALU.mult, ALU.add))
                wait()
                did(eng.scalar_tensor_tensor(lo, w, SW, hi, ALU.mult, ALU.subtract))
            for k in range(U):
                eng.wait_ge(s_scat[k], 16)
            fbv = xr[0][:, 0, 0:E1 * 2 * HC].rearrange("p (e c) -> p e c", e=E1)
            did(eng.tensor_scalar(fb[:, :, 0:HC], fbv[:, :, 0:HC], 0.5, 0.0, ALU.mult, ALU.add))
            did(eng.tensor_scalar(fb[:, :, HC:2 * HC], fbv[:, :, 0:HC], 0.5 * SX / SZ, 0.0, ALU.mult, ALU.add))
            did(eng.tensor_scalar(fb[:, :, 2 * HC:3 * HC], fbv[:, :, HC:2 * HC], SZ, 0.0, ALU.mult, ALU.add))
            eng.wait_ge(s_up, 1)
            for l in range(2):
                for k in range(KC):
                    did(eng.tensor_copy(u_src[:, l, k, :], psm[:, 4 * l + 2 * k:4 * l + 2 * k + 1]))
                    did(eng.tensor_copy(u_dst[:, l, k, :], psm[:, 4 * l + 2 * k + 1:4 * l + 2 * k + 2].to_broadcast([P, P])))
            wait()
            eng.memset(zero8[:, :], 0.0).then_inc(s_setup, 1)
            assert st.n == DVE_SETUP, st.n
            eng.wait_ge(s_setup, 2)

            with eng.Fori(0, TURNS) as i:
                st = Steps(eng, s_dve, DVE_TURN, i)
                st.base = DVE_SETUP
                did, wait = st.did, st.wait

                def bc(x, n):
                    return x.unsqueeze(2).to_broadcast([P, T, n])

                def norm_stats(j):
                    for u in range(U):
                        x = xin[u] if j == 0 else xr[u]
                        if j == 0:
                            eng.wait_ge(s_x[u], at(i, 16, 16))
                        else:
                            eng.wait_ge(s_xr, at(i, XR_FIRST, XR_FIRST + (j - 1) * U + u + 1))
                        for t in range(T):
                            did(eng.bn_stats(stats[:, u, t, :], x[:, t, :]))
                        st.hold()
                        for t in range(T):
                            ins = eng.bn_aggr(mv[:, u, t, :], stats[:, u, t, :])
                        ins.then_inc(s_var, 1)

                def norm_apply(j):
                    for u in range(U):
                        x = xin[u] if j == 0 else xr[u]
                        o = pay[u] if j == 3 else xn[u]
                        eng.wait_ge(s_rstd, at(i, 4 * U, j * U + u + 1))
                        if j == 3:
                            eng.wait_ge(s_scat[u], at(i, 2 * T * 16, 16))
                        for t in range(T):
                            eng.tensor_scalar(o[:, t, 0:D], x[:, t, :], mv[:, u, t, 0:1], rstd[:, u, t:t + 1],
                                              ALU.subtract, ALU.mult).then_inc(s_xn, 1)

                def elu(l):
                    for u in range(U):
                        for h in range(H):
                            k = MM[("attn", l, u, h)]
                            eng.wait_ge(s_elu, at(i, 2 * U * T, (l * U + u) * T + 2 * h + 2))
                            for t2 in range(2):
                                ins = eng.tensor_scalar(SE[u][:, h, 1, t2 * D:(t2 + 1) * D], pmm[k % NMM][:, t2 * D:(t2 + 1) * D],
                                                        rinv[:, u, 2 * h + t2:2 * h + t2 + 1], 0.0, ALU.mult, ALU.max)
                            ins.then_inc(s_relu, 1)
                        eng.wait_ge(s_relu, at(i, 2 * U * H, (l * U + u + 1) * H))
                        r = SE[u][:, :, 1, :]
                        did(eng.scalar_tensor_tensor(r, SE[u][:, :, 0, :], 1.0, r, ALU.min, ALU.add))
                        wait()
                        o = xr[u][:, :, :].rearrange("p (h t) d -> p h (t d)", h=H)
                        x = (xin[u] if l == 0 else xr[u])[:, :, :].rearrange("p (h t) d -> p h (t d)", h=H)
                        if l == 0:
                            eng.wait_ge(s_store[u], at(i, 16, 16))
                        eng.scalar_tensor_tensor(o, r, -1.0, x, ALU.add, ALU.add).then_inc(s_xr, 1)

                def gnn(l):
                    norm_stats(2 * l)
                    norm_apply(2 * l)
                    for u in range(U):
                        if l == 0:
                            eng.wait_ge(s_link, at(i, U, 2 + u))
                        eng.wait_ge(s_srcp, at(i, 2 * U, l * U + u + 1))
                        did(eng.tensor_copy(src[:, u, :], SRC[u]))
                        hold(eng, s_f, at(i, 2 * U, l * U + u + 1))
                        for t in range(T):
                            eng.tensor_tensor_reduce(out=S[u][:, t, :], in0=pf[:, :], in1=link[u][:, t, :], scale=1.0,
                                                     scalar=4 * NOT_LINKED, op0=ALU.add, op1=ALU.max,
                                                     accum_out=mrow[:, u, t:t + 1]).then_inc(s_sc, 1)
                        eng.wait_ge(s_sc, at(i, 2 * U * T, (l * U + u + 1) * T))
                        wait()
                        did(eng.tensor_tensor(mrow[:, u, :], mrow[:, u, :], src[:, u, :], ALU.add))
                        wait()
                        did(eng.scalar_tensor_tensor(mx[:, u, :], mrow[:, u, :], SLOPE, mrow[:, u, :], ALU.mult, ALU.max))
                        wait()
                        did(eng.tensor_tensor(b1[:, u, :], src[:, u, :], mx[:, u, :], ALU.subtract))
                        eng.scalar_tensor_tensor(b2[:, u, :], src[:, u, :], SLOPE, mx[:, u, :], ALU.mult, ALU.subtract).then_inc(s_mxr, 1)
                        if l:
                            rest = xn[u][:, 0:2, :].rearrange("p a b -> p (a b)")
                            for t in range(T):
                                did(eng.max(top[:, u, t, :], S[u][:, t, :]))
                                st.hold()
                                did(eng.match_replace(rest, top[:, u, t, :], S[u][:, t, :], 2 * NOT_LINKED))
                                st.hold()
                                did(eng.max(top2[:, u, t, :], rest))
                    for u in range(U):
                        for t in range(T):
                            eng.wait_ge(s_p, at(i, 4 * U * T, ((l * U + u) * T + t + 1) * 2))
                            s, q = S[u][:, t, :], stage[ST[("p", l, u, t, 0)] % NST][:, :]
                            if l == 0:
                                eng.scalar_tensor_tensor(s, q, 1.0, s, ALU.mult, ALU.max, accum_out=rs[:, u, t:t + 1]).then_inc(s_keep, 1)
                            else:
                                did(eng.scalar_tensor_tensor(q, q, 1.0, stage[ST[("p", l, u, t, 1)] % NST][:, :], ALU.mult, ALU.max,
                                                             accum_out=rs[:, u, t:t + 1]))
                                wait()
                                eng.scalar_tensor_tensor(s, s, top2[:, u, t, 7:8], q, ALU.is_ge, ALU.mult).then_inc(s_keep, 1)
                        eng.wait_ge(s_keep, at(i, 2 * U * T, (l * U + u + 1) * T))
                        eng.reciprocal(rinv[:, u, :], rs[:, u, :]).then_inc(s_rinv, 1)
                    eng.wait_ge(s_rinv, at(i, 2 * U, (l + 1) * U))
                    elu(l)

                def gates(j, u, ne, gate, scale):
                    wait()
                    hold(eng, s_lgr, at(i, 2 * U, j * U + u + 1))
                    for t in range(T):
                        did(eng.max(m8[:, u, t, :], lg[:, u, t, :]))
                    st.hold()
                    for t in range(T):
                        did(eng.max_index(i8[:, u, t, :], m8[:, u, t, :], lg[:, u, t, :]))
                    eng.tensor_tensor(dif[:, u, :], m8[:, u, :, 1], m8[:, u, :, 0], ALU.subtract).then_inc(s_dif, 1)
                    wait()
                    did(eng.tensor_copy(i8f[:, u, :, :], i8[:, u, :, 0:2]))
                    wait()
                    it = iota8.unsqueeze(1).to_broadcast([P, T, 8])
                    did(eng.tensor_tensor(oh1[:, u, :, :], it, bc(i8f[:, u, :, 0], 8), ALU.is_equal))
                    did(eng.tensor_tensor(oh2[:, u, :, :], it, bc(i8f[:, u, :, 1], 8), ALU.is_equal))
                    return lambda: gates_end(j, u, gate, scale)

                def gates_end(j, u, gate, scale):
                    eng.wait_ge(s_e2, at(i, 2 * U, j * U + u + 1))
                    did(eng.tensor_scalar(den[:, u, :], e2[:, u, :], 1.0 / scale, 1.0 / scale, ALU.mult, ALU.add))
                    wait()
                    did(eng.reciprocal(w1[:, u, :], den[:, u, :]))
                    wait()
                    did(eng.tensor_tensor(w2[:, u, :], e2[:, u, :], w1[:, u, :], ALU.mult))
                    did(eng.tensor_tensor(g1[:, u, :, :], oh1[:, u, :, :], bc(w1[:, u, :], 8), ALU.mult))
                    wait()
                    did(eng.tensor_tensor(g2[:, u, :, :], oh2[:, u, :, :], bc(w2[:, u, :], 8), ALU.mult))
                    wait()
                    did(eng.tensor_tensor(gate, g1[:, u, :, :], g2[:, u, :, :], ALU.add))
                    wait()

                gnn(0)
                norm_stats(1)
                norm_apply(1)
                for u in range(U):
                    for h in range(H):
                        k = TR[("xn", 1, u, h)]
                        eng.wait_ge(s_xh, at(i, U * H, u * H + h + 1))
                        n = slice(h * 2 * P, (h + 1) * 2 * P)
                        eng.scalar_tensor_tensor(xh[u][:, 1, :, n], ptr[k % NTR][:, :].rearrange("p (k n) -> p k n", k=KC), SX,
                                                 xh[u][:, 0, :, n], ALU.mult, ALU.subtract)\
                           .then_inc(s_xl, 1)
                ends = []
                for u in range(U):
                    eng.wait_ge(s_lgp, at(i, 2 * U, u + 1))
                    if u == 0:
                        wait()
                        did(eng.memset(lg[:, :, :, E0:8], NOT_LINKED))
                    eng.scalar_tensor_tensor(lg[:, u, :, 0:E0], LG0[u], 1.0 / SZ, rb0[:, :].unsqueeze(1).to_broadcast([P, T, E0]),
                                             ALU.mult, ALU.add).then_inc(s_lgr, 1)
                    ends.append(gates(0, u, E0, gate0[:, u, :, :], 0.5 / SZ))
                    for t in range(T):
                        for g in range(2):
                            k, q = MM[("z", u, t, g)], ST[("z", u, t, g)]
                            z = stage[q % NST]
                            eng.wait_ge(s_tanh, at(i, 2 * U * T, (u * T + t) * 2 + g + 1))
                            eng.scalar_tensor_tensor(z[:, :], z[:, :], 1.0, pmm[k % NMM][:, :], ALU.add, ALU.mult).then_inc(s_zact, 1)
                            if t == 0 and g == 0:
                                ends[u]()
                            wait()
                            eng.wait_ge(s_zact, at(i, 2 * U * T, (u * T + t) * 2 + g + 1))
                            for e in range(2):
                                ex = 2 * g + e
                                gt = gate0[:, u, t, ex:ex + 1]
                                o = comb[u][:, t, :]
                                if ex == 0:
                                    ins = eng.tensor_scalar(o, z[:, e * D:(e + 1) * D], gt, 0.0, ALU.mult, ALU.add)
                                else:
                                    ins = eng.scalar_tensor_tensor(o, z[:, e * D:(e + 1) * D], gt, o, ALU.mult, ALU.add)
                                if e == 1:
                                    ins.then_inc(s_stfree, 1)
                                    if g == 0:
                                        eng.wait_ge(s_stfree, at(i, 2 * U * T, (u * T + t) * 2 + 1))
                                else:
                                    did(ins)
                                    wait()
                for u in range(U):
                    for h in range(H):
                        k = MM[("out", u, h)]
                        eng.wait_ge(s_mmf, at(i, MM_PER, k + 1))
                        v = slice(2 * h, 2 * h + 2)
                        eng.tensor_tensor(comb[u][:, v, :].rearrange("p t d -> p (t d)"), pmm[k % NMM][:, :],
                                          xn[u][:, v, :].rearrange("p t d -> p (t d)"), ALU.add)\
                           .then_inc(s_y, 1)
                for u in range(U):
                    eng.wait_ge(s_rr, at(i, U, u + 1))
                    for t in range(T):
                        did(eng.scalar_tensor_tensor(comb[u][:, t, :], comb[u][:, t, :], rr[:, u, t:t + 1], nw[:, :], ALU.mult, ALU.mult))
                    wait()
                    eng.tensor_tensor(xr[u][:, :, :], xr[u][:, :, :], comb[u][:, :, :], ALU.add).then_inc(s_xr, 1)
                gnn(1)
                norm_stats(3)
                norm_apply(3)
                ends = []
                for u in range(U):
                    eng.wait_ge(s_lgp, at(i, 2 * U, U + u + 1))
                    eng.tensor_tensor(lg[:, u, :, :], LG1[u], rb1[:, :].unsqueeze(1).to_broadcast([P, T, E1]), ALU.add).then_inc(s_lgr, 1)
                    ends.append(gates(1, u, E1, pay[u][:, :, D:D + E1], 1.0 / SZ))
                    wait()
                    eng.tensor_tensor(chose[:, u, :, :], oh1[:, u, :, :], oh2[:, u, :, :], ALU.add).then_inc(s_chose, 1)
                for u in range(U):
                    ends[u]()
                    did(eng.tensor_copy(pay[u][:, :, ROW - 1:ROW].rearrange("p t o -> p (t o)").bitcast(I32), tokf[:, u, :]))
                    eng.wait_ge(s_pos, at(i, U, U))
                    did(eng.tensor_tensor(place[:, u, :, :], POS[u], base[:, :].unsqueeze(1).to_broadcast([P, T, E1]), ALU.add))
                    wait()
                    did(eng.tensor_tensor(g1[:, u, :, :], place[:, u, :, :], oh1[:, u, :, :], ALU.mult))
                    did(eng.tensor_tensor(g2[:, u, :, :], place[:, u, :, :], oh2[:, u, :, :], ALU.mult))
                    did(eng.tensor_tensor(base[:, :], TOT[u], base[:, :], ALU.add))
                    did(eng.tensor_scalar(tokf[:, u, :], tokf[:, u, :], float(U * N), 0.0, ALU.add, ALU.add))
                    wait()
                    did(eng.tensor_reduce(slotf[:, u, 0, :], g1[:, u, :, :], AX.X, ALU.add))
                    did(eng.tensor_reduce(slotf[:, u, 1, :], g2[:, u, :, :], AX.X, ALU.add))
                    wait()
                    eng.tensor_copy(slot[:, u, :, :], slotf[:, u, :, :]).then_inc(s_slot, 1)
                assert st.n == DVE_TURN, st.n

            st = Steps(eng, s_dve, 0, 0)
            st.base = DVE_SETUP + TURNS * DVE_TURN
            did, wait = st.did, st.wait
            did(eng.memset(pad, 0.0))
            did(eng.tensor_copy(basei[:, :], base[0:1, :]))
            did(eng.tensor_tensor(tilesf[:, :], base[0:1, :], ebase[0:1, :], ALU.subtract))
            wait()
            did(eng.tensor_scalar(tilesf[:, :], tilesf[:, :], float(SLOTS - 1), 0.0, ALU.add, ALU.add))
            wait()
            did(eng.tensor_copy(pad[:, :, ROW - 1:ROW].rearrange("p s o -> p (s o)").bitcast(I32), padtok))
            did(eng.tensor_copy(cnti[:, :], tilesf[:, :]))
            wait()
            did(eng.tensor_scalar(cnti[:, :], cnti[:, :], SLOTS.bit_length() - 1, None, ALU.arith_shift_right))
            wait()
            did(eng.tensor_copy(tilesf[:, :], cnti[:, :]))
            wait()
            did(eng.tensor_tensor_scan(tcum[:, :], tilesf[:, :], zero8[:, :], 0.0, ALU.add, ALU.add))
            did(eng.memset(tex, 0.0))
            did(eng.memset(tst, 0.0))
            wait()
            for e in range(E1):
                did(eng.tensor_scalar(tge, jnum, tcum[:, e:e + 1], tilesf[:, e:e + 1], ALU.is_ge, ALU.mult))
                did(eng.scalar_tensor_tensor(tex, jnum, tcum[:, e:e + 1], tex, ALU.is_ge, ALU.add))
                wait()
                did(eng.tensor_tensor(tst, tst, tge, ALU.add))
                wait()
            did(eng.tensor_tensor(tst, jnum, tst, ALU.subtract))
            did(eng.tensor_scalar(tge, tex, float(REGION), 0.0, ALU.mult, ALU.add))
            wait()
            did(eng.scalar_tensor_tensor(tst, tst, float(SLOTS), tge, ALU.mult, ALU.add))
            wait()
            did(eng.tensor_scalar(tst, tst, float(E1 * REGION), 0.0, ALU.min, ALU.max))
            did(eng.tensor_scalar(tex, tex, float(E1 - 1), 0.0, ALU.min, ALU.max))
            wait()
            did(eng.tensor_copy(tile_row[:, :], tst))
            wait()
            eng.tensor_copy(tile_expert[:, :], tex).then_inc(s_table, 1)
            did(eng.memset(ah[1], 0.0))
            did(eng.memset(al[1], 0.0))
            did(eng.memset(gsel[:, 1, :], 0.0))
            did(eng.tensor_copy(tsel[:, 1, :], padtok))
            wait()
            eng.nop().then_inc(s_table, 1)
            eng.wait_ge(s_table, 2)
            eng.sem_inc(s_al, 1)

            def lo(v):
                eng.scalar_tensor_tensor(gxh[v][:, 1, :, :], ptr[v][:, :].rearrange("p (k n) -> p k n", k=KC), SX,
                                         gxh[v][:, 0, :, :], ALU.mult, ALU.subtract).then_inc(s_gxl, 1)
            eng.wait_ge(s_gxh, 1)
            lo(0)
            with eng.Fori(0, TILES // 2) as i:
                for v in range(2):
                    q = 1 - v
                    e = eng.value_load(tile_expert[0:1, bass.ds(i * 2 + v + 1, 1)], min_val=0, max_val=E1 - 1)
                    eng.tensor_copy(bsel[:, v, :], fb[:, bass.ds(e, 1), :].rearrange("p e c -> p (e c)")).then_inc(s_bsel, 1)
                    eng.wait_ge(s_bsel, at(i, 2, v + 1))
                    for c in range(HC):
                        eng.wait_ge(s_th, at(i, 4 * HC, (v * HC + c + 1) * 2))
                        eng.scalar_tensor_tensor(th[c], th[c], 1.0, z1[c], ALU.add, ALU.mult).then_inc(s_silu, 1)
                        eng.wait_ge(s_silu, at(i, 2 * HC, v * HC + c + 1))
                        eng.scalar_tensor_tensor(av[c], pmm[c][:, SLOTS:2 * SLOTS], bsel[:, v, 2 * HC + c:2 * HC + c + 1], th[c],
                                                 ALU.add, ALU.mult).then_inc(s_av, 1)
                        if c >= 1:
                            eng.wait_ge(s_ah, at(i, 2 * HC, v * HC + c))
                            eng.tensor_tensor(al[v][:, c - 1, :], av[c - 1], ah[v][:, c - 1, :], ALU.subtract).then_inc(s_al, 1)
                    eng.wait_ge(s_gxh, at(i, 2, v + 2))
                    lo(q)
                    eng.wait_ge(s_ah, at(i, 2 * HC, v * HC + HC))
                    eng.tensor_tensor(al[v][:, HC - 1, :], av[HC - 1], ah[v][:, HC - 1, :], ALU.subtract).then_inc(s_al, 1)
                    eng.wait_ge(s_gx[v], at(i, 16, 16))
                    eng.wait_ge(s_add, at(i, 64, 48 + 32 * v))
                    eng.tensor_copy(tsel[:, v, :], gx[v][:, :, ROW - 1:ROW].rearrange("p s o -> p (s o)").bitcast(I32))
                    eng.tensor_copy(gsel[:, v, :], gx[v][:, :, bass.ds(e + D, 1)].rearrange("p s o -> p (s o)")).then_inc(s_sel, 1)



def kernel(**inputs):
    import concourse.bacc as bacc
    from concourse.bass_utils import run_bass_kernel_spmd

    f = {k: np.ascontiguousarray(v) for k, v in inputs.items()}

    def rep(v):
        return np.ascontiguousarray(np.broadcast_to(v.reshape(1, -1), (P, v.size)))

    cst = np.zeros((P, 22 + TABLE), np.float32)
    cst[:, 0:8] = np.arange(8)
    cst[:, 8:8 + T] = np.arange(P)[:, None] + P * np.arange(T)
    cst[:, 12:20] = REGION * np.arange(E1)
    cst[:, 20:22] = TOK + np.arange(P)[:, None] + P * np.arange(2)
    cst[:, 22:] = np.arange(TABLE) - 1
    arrays = {
        "x": f["x"].reshape(TOK, D),
        "adj": f["adj"].reshape(TOK, N),
        "ident": np.eye(P, dtype=np.float32),
        "before": np.triu(np.ones((P, P), np.float32), 1),
        "cst": cst,
        "nw": rep(f["L0_ffn_norm_w"]),
        "rb0": rep(f["L0_ffn_router_b"]),
        "rb1": rep(f["L1_ffn_router_b"]),
        "rw0": f["L0_ffn_router_w"],
        "rw1": np.ascontiguousarray(f["L1_ffn_router_w"].T),
        "a0": np.concatenate([f["L0_gnn_a1"], f["L0_gnn_a2"]], 1),
        "a1": np.ascontiguousarray(f["L1_gnn_a"].reshape(2, D).T),
        "gw0t": f["L0_gnn_W"],
        "gw1t": np.ascontiguousarray(f["L1_gnn_W"].T),
        "gw1": f["L1_gnn_W"],
        "ow": f["L0_ffn_out_w"],
        "ew": np.ascontiguousarray(f["L0_ffn_expert_w"].transpose(1, 0, 2)).reshape(D, E0 * D),
        "fb1": np.ascontiguousarray(f["L1_ffn_fc1_b"].reshape(E1 * 2 * HC, P).T),
        "brow": np.concatenate([f["L0_ffn_expert_b"].ravel(), f["L0_ffn_out_b"], f["L1_ffn_fc2_b"].ravel()]).reshape(P, -1),
        "f1": np.ascontiguousarray(f["L1_ffn_fc1_w"].transpose(0, 2, 1)),
        "f2": np.ascontiguousarray(f["L1_ffn_fc2_w"].transpose(0, 2, 1)),
    }
    nc = bacc.Bacc("TRN2", target_bir_lowering=False, num_devices=1, dynamic_dma_scratch_size=8192)
    a = {k: nc.dram_tensor(f"in_{k}", v.shape, mybir.dt.from_np(v.dtype), kind="ExternalInput").ap() for k, v in arrays.items()}
    a.update(COUNTS)
    out = nc.dram_tensor("out", [TOK + SLOTS, D], F32, kind="ExternalOutput").ap()
    build(nc, a, out)
    r = run_bass_kernel_spmd(nc, [{f"in_{k}": v for k, v in arrays.items()}], core_ids=[0])
    return r.results[0]["out"][0:TOK, :].reshape(B, N, D)


COUNTS = {"dve_setup": 25, "dve_turn": 193, "pool_setup": 0, "pool_turn": 16}
```

```python
import numpy as np
import concourse.bass as bass
from concourse import mybir
from contextlib import ExitStack

F32 = mybir.dt.float32
F16 = mybir.dt.float16
BF16 = mybir.dt.bfloat16
I32 = mybir.dt.int32
U32 = mybir.dt.uint32
ALU = mybir.AluOpType
ACT = mybir.ActivationFunctionType
AX = mybir.AxisListType

P = 128
B, N, D = 16, 512, 256
T = N // P
KC = D // P
H = T // 2
E0 = 4
E1 = 8
HID = 512
HC = HID // P
TOK = B * N
BANK = 512
U = 2
TURNS = B // U

SLOTS = 2 * P
REGION = TOK + SLOTS
ROW = D + E1 + 1
TILES = 2 * TOK // SLOTS + E1
TABLE = TILES + 3

SX = 16.0
SW = 64.0
SZ = SX * SW
NOT_LINKED = -2.0 ** 100
LN_EPS = 1e-05
RMS_EPS = 1e-06
SLOPE = 0.2

FIRST = (["stats0", "xn0", "link", "xt0", "f0", "scores0"] + [f"keep0t{t}" for t in range(T)]
         + ["pt0", "attn0h0", "elu0h0", "attn0h1", "elu0h1", "send", "split0", "stats1", "xn1", "xh1", "xl1", "logits0", "top0"]
         + [f"z{t}" for t in range(T)] + ["split1"])
SECOND = (["comb", "out", "y", "x2h0", "x2h1", "stats2", "split2", "xn2", "xt2", "f1", "wh", "scores1"]
          + [f"kth{h}" for h in range(H)] + [f"keep1t{t}" for t in range(T)]
          + ["pt1", "attn1h0", "elu1h0", "attn1h1", "elu1h1", "stats3", "xn3", "xt3", "logits1", "top1", "choice",
             "slots", "store"])

def runs(first, text):
    return [((first + k) % 2, name) for k, run in enumerate(text.split("|")) for name in run.split()]


CYCLE = {
    "tensor": runs(1, """
        comb out | xn0 f0 | xn2 f1 | keep0t0 keep0t1 keep0t2 keep0t3 attn0h0 attn0h1 | wh keep1t0 | xn1 |
        keep1t1 | logits0 z0 | keep1t2 | z1 | keep1t3 attn1h0 attn1h1 | z2 z3 | xn3 logits1 choice"""),
    "vector": runs(0, """
        stats0 xn0 | y x2h0 x2h1 stats2 xn2 | scores0 keep0t0 keep0t1 | scores1 | keep0t2 keep0t3 | kth0 kth1 |
        elu0h0 elu0h1 stats1 | keep1t0 | xn1 | keep1t1 | xl1 | keep1t2 | logits0 top0 | keep1t3 | z0 z1 |
        elu1h0 elu1h1 stats3 | z2 | xn3 | z3 | logits1 top1 slots"""),
    "scalar": runs(1, """
        comb y | xt0 | xt2 | scores0 keep0t2 keep0t3 pt0 attn0h0 attn0h1 | wh scores1 keep1t1 | xh1 |
        keep1t2 keep1t3 | top0 z0 | pt1 | z1 | attn1h0 attn1h1 | z2 z3 | xt3 top1 store"""),
    "gpsimd": runs(0, """
        stats0 | x2h0 x2h1 | link | stats2 | send split0 stats1 split1 | split2 stats3"""),
}

BANKS = ([("xn", 0, h) for h in range(H)] + [("src", 0), ("f", 0)] + [("p", 0, t) for t in range(T)]
         + [("attn", 0, h) for h in range(H)] + [("xn", 1, h) for h in range(H)] + [("logits", 0)]
         + [("z", t, g) for t in range(T) for g in range(2)]
         + [("comb", h) for h in range(H)] + [("out", h) for h in range(H)]
         + [("xn", 2, h) for h in range(H)] + [("src", 1), ("f", 1)] + [("wh", h) for h in range(H)]
         + [("p", 1, t) for t in range(T)] + [("attn", 1, h) for h in range(H)]
         + [("xn", 3, h) for h in range(H)] + [("logits", 1)])
STAGED = ([("p", 0, t, 0) for t in range(T)] + [("z", t, g) for t in range(T) for g in range(2)]
          + [("p", 1, t, k) for t in range(T) for k in range(2)])
NB_RING, NST = 4, 2
assert len(BANKS) % NB_RING == 0 and len(STAGED) % NST == 0
BANK_AT = {k: n for n, k in enumerate(BANKS)}
STAGE_AT = {k: n for n, k in enumerate(STAGED)}


def build(nc, a, out):
    ctx = ExitStack()
    with ctx:
        def sb(name, shape, dt=F32):
            return ctx.enter_context(nc.sbuf_tensor(name, shape, dt))

        def sem(name):
            return ctx.enter_context(nc.semaphore(name))

        def sems(name, n):
            return [sem(f"{name}{k}") for k in range(n)]

        ident = sb("ident", [P, P])
        before = sb("before", [P, P], BF16)
        ones = sb("ones", [P, P], BF16)
        unscale = sb("unscale", [3, P], BF16)
        cst = sb("cst", [P, a["cst"].shape[1]])
        iota8, tok0, ebase, padtok = cst[:, 0:8], cst[:, 8:8 + T], cst[:, 12:20], cst[:, 20:22]
        jnum = cst[0:1, 22:22 + TABLE]
        nw = sb("nw", [P, D])
        rb0, rb1 = sb("rb0", [P, E0]), sb("rb1", [P, E1])
        rw1 = sb("rw1", [P, KC, E1])
        w0a, w1a = sb("w0a", [P, KC, 2]), sb("w1a", [P, KC, 2])
        u_src, u_dst = sb("u_src", [P, 2, KC, 1]), sb("u_dst", [P, 2, KC, P])
        gw1 = sb("gw1", [P, KC, D])
        ow = sb("ow", [P, KC, D])
        ewh, ewl = sb("ewh", [P, KC, E0 * D], F16), sb("ewl", [P, KC, E0 * D], F16)
        rwh, rwl = sb("rwh", [P, KC, E0], F16), sb("rwl", [P, KC, E0], F16)
        NB = E0 * D + D + E1 * D
        BSP = NB // P
        NB0 = E0 * D + D
        brow = sb("brow", [3, NB0], BF16)
        brow2 = ewh[0:3, :, :].rearrange("p k f -> p (k f)").bitcast(BF16)
        f1h, f1l = sb("f1h", [P, E1, KC, 2 * HID], F16), sb("f1l", [P, E1, KC, 2 * HID], F16)
        f2h, f2l = sb("f2h", [P, E1, HC, D], F16), sb("f2l", [P, E1, HC, D], F16)
        fb = sb("fb", [P, E1, 3 * HC])
        wst = sb("wst", [P, 2 * HID])

        adj = sb("adj", [P, T, N], I32)
        xin = [sb(f"xin{u}", [P, T, D]) for u in range(U)]
        xr = [sb(f"xr{u}", [P, T, D]) for u in range(U)]
        link = [sb(f"link{u}", [P, T, N], BF16) for u in range(U)]
        xn = [sb(f"xn{u}", [P, T, D]) for u in range(U)]
        xt = [sb(f"xt{u}", [P, KC, N]) for u in range(U)]
        S = [sb(f"S{u}", [P, T, N]) for u in range(U)]
        PT = [S[u][:, :, :].rearrange("p t (m n) -> p t m n", m=T) for u in range(U)]
        comb = [sb(f"comb{u}", [P, T, D]) for u in range(U)]
        pay = [sb(f"pay{u}", [P, T, ROW]) for u in range(U)]
        xh = [S[u][:, 0:2, :].rearrange("p a b -> p (a b)").bitcast(F16)
              .rearrange("p (s k n) -> p s k n", s=2, k=KC) for u in range(U)]
        stage = [[sb(f"stage{u}{k}", [P, BANK]) for k in range(NST)] for u in range(U)]
        SE = [S[u][:, :, :].rearrange("p (h two) n -> p h two n", two=2) for u in range(U)]

        stats, mv = sb("stats", [P, U, T, 6]), sb("mv", [P, U, T, 2])
        rstd, ve, mhalf = sb("rstd", [P, U, T]), sb("ve", [P, U, T]), sb("mhalf", [P, T])
        src = sb("src", [P, U, T])
        mrow, mx, b1, b2 = (sb(n, [P, U, T]) for n in ("mrow", "mx", "b1", "b2"))
        top, top2 = sb("top", [P, U, T, 8]), sb("top2", [P, U, T, 8])
        rs, rinv = sb("rs", [P, U, T]), sb("rinv", [P, U, T])
        ss, rr = sb("ss", [P, U, T]), sb("rr", [P, U, T])
        lg, m8, i8 = sb("lg", [P, U, T, 8]), sb("m8", [P, U, T, 8]), sb("i8", [P, U, T, 8], U32)
        i8f = sb("i8f", [P, U, T, 2])
        dif, e2, den = sb("dif", [P, U, T]), sb("e2", [P, U, T]), sb("den", [P, U, T])
        w1, w2 = sb("w1", [P, U, T]), sb("w2", [P, U, T])
        oh1, oh2 = sb("oh1", [P, U, T, 8]), sb("oh2", [P, U, T, 8])
        g1, g2 = sb("g1", [P, U, T, 8]), sb("g2", [P, U, T, 8])
        gate0 = sb("gate0", [P, U, T, 8])
        chose = sb("chose", [P, U, T, 8], BF16)
        place = sb("place", [P, U, T, 8])
        slotf, slot = sb("slotf", [P, U, 2, T]), sb("slot", [P, U, 2, T], I32)
        base, tokf = sb("base", [P, E1]), sb("tokf", [P, U, T])
        pad = xin[0][:, :, :].rearrange("p t d -> p (t d)")[:, 0:2 * ROW].rearrange("p (s r) -> p s r", s=2)
        basei, cnti, tilesf, tcum = sb("basei", [1, E1], I32), sb("cnti", [1, E1], I32), sb("tilesf", [1, E1]), sb("tcum", [1, E1])
        zero8 = sb("zero8", [1, E1])
        tex, tst, tge = (xin[1][0:1, k, 0:TABLE] for k in range(3))
        tile_expert, tile_row = sb("tile_expert", [1, TABLE], I32), sb("tile_row", [1, TABLE], I32)
        gx = [pay[u][:, 0:2, :] for u in range(2)]
        gxh = [xt[u][:, 0, :].bitcast(F16).rearrange("p (s k n) -> p s k n", s=2, k=KC) for u in range(2)]
        ah = [xn[u][:, 0:2, :].rearrange("p a b -> p (a b)").bitcast(F16).rearrange("p (c n) -> p c n", c=HC) for u in range(2)]
        al = [xn[u][:, 2:4, :].rearrange("p a b -> p (a b)").bitcast(F16).rearrange("p (c n) -> p c n", c=HC) for u in range(2)]
        th = [S[0][:, c, 0:SLOTS] for c in range(HC)]
        z1 = [S[0][:, c, SLOTS:2 * SLOTS] for c in range(HC)]
        av = [S[1][:, c, 0:SLOTS] for c in range(HC)]
        ys = [comb[u][:, 0:2, :] for u in range(2)]
        gsel, tsel = sb("gsel", [P, 2, 2]), sb("tsel", [P, 2, 2], I32)
        bsel = sb("bsel", [P, 2, 3 * HC])

        def bank(name):
            return ctx.enter_context(nc.psum_tensor(name, [P, BANK], F32))
        bank8 = [bank(f"bank{k}") for k in range(8)]
        banks = [bank8[0:NB_RING], bank8[NB_RING:]]
        POS, TOT = slice(32, 64), slice(64, 72)
        ptr, pmm, pf, psm = bank8[0:2], bank8[2:6], bank8[6], bank8[7]

        rows = nc.dram_tensor("rows", [E1 * REGION + SLOTS, ROW], F32, kind="Internal").ap()
        parts_d = nc.dram_tensor("parts_d", [3, NB], BF16, kind="Internal").ap()
        x_v = a["x"].rearrange("(b t p) d -> b p t d", p=P, t=T)
        adj_v = a["adj"].rearrange("(b t p) m -> b p t m", p=P, t=T)
        out_v = out[0:TOK, :].rearrange("(b t p) d -> b p t d", p=P, t=T)
        f1_v = a["f1"].rearrange("e (k p) f -> e p k f", p=P)
        f2_v = a["f2"].rearrange("e (k p) f -> e p k f", p=P)

        s_const = sem("consts_loaded")
        s_wld = sem("weights_loaded")
        s_bst, s_bl = sem("bias_rows_stored"), sem("bias_rows_loaded")
        s_setup = sem("setup_done")
        s_gs = sem("gpsimd_setup")
        s_up = sem("u_products")
        s_x = sems("x_loaded", U)
        s_adj = sems("adj_loaded", U)
        s_link = sems("link_ready", U)
        s_var = sems("variance_ready", U)
        s_rstd = sems("rstd_ready", U)
        s_xn = sems("xn_ready", U)
        s_bank = sems("bank_filled", U)
        s_relu = sems("attention_bank_read", U)
        s_zact = sems("expert_bank_read", U)
        s_xt = sems("xt_ready", U)
        s_xh = sems("xhi_ready", U)
        s_xl = sems("xlo_ready", U)
        s_sc = sems("scores_ready", U)
        s_mxr = sems("max_ready", U)
        s_p = sems("exp_ready", U)
        s_keep = sems("kept_ready", U)
        s_pt = sems("pt_ready", U)
        s_wh = sems("wh_ready", U)
        s_elu = sems("elu_exp_ready", U)
        s_rinv = sems("rinv_ready", U)
        s_xr = sems("x_updated", U)
        s_lgr = sems("logits_read", U)
        s_dif = sems("top2_gap_ready", U)
        s_e2 = sems("top2_exp_ready", U)
        s_tanh = sems("tanh_ready", U)
        s_stfree = sems("stage_used", U)
        s_y = sems("y_ready", U)
        s_ssq = sems("square_sum_ready", U)
        s_rr = sems("rms_ready", U)
        s_chose = sems("choice_ready", U)
        s_pos = sems("positions_ready", U)
        s_slot = sems("slots_ready", U)
        s_base = sem("expert_fill_updated")
        s_scat = sems("rows_scattered", U)
        s_store = sems("x_stored", U)
        s_wst = sem("expert_weights_loaded")
        s_wsp = sem("expert_weights_split")
        s_dve = sems("dve_step", U + 1)
        s_pool = sems("pool_step", U)
        s_held = sem("held")
        s_table = sem("tile_table_ready")
        s_padw = sem("padding_written")
        s_gx = sems("rows_loaded", 2)
        s_gtr = sem("rows_transposed")
        s_gxh = sem("rows_hi_ready")
        s_gxl = sem("rows_lo_ready")
        s_bsel = sem("tile_biases_selected")
        s_sel = sem("tile_columns_selected")
        s_h = sem("hidden_ready")
        s_th = sem("hidden_act_ready")
        s_silu = sem("silu_ready")
        s_av = sem("gated_ready")
        s_ah = sem("gated_hi_ready")
        s_al = sem("gated_lo_ready")
        s_yp = sem("expert_out_ready")
        s_ys = sem("expert_out_scaled")
        s_add = sem("expert_out_added")

        def at(i, per, n):
            if isinstance(i, tuple):
                return i[0] * per + (i[1] * per + n)
            return i * per + n

        NBANK, XR_FIRST = len(BANKS), 3 * H

        def bank_read(k):
            if k[0] == "p":
                return s_pt, 2 * T, k[1] * T + k[2] + 1
            if k[:2] == ("xn", 1):
                return s_xl, H, k[2] + 1
            if k[0] in ("xn", "comb"):
                use = 1 if k[0] == "comb" else k[1]
                return s_xt, 4 * H, use * H + k[-1] + 1
            if k[0] == "src":
                return s_mxr, 2, k[1] + 1
            if k[0] == "f":
                return s_sc, 2 * T, (k[1] + 1) * T
            if k[0] == "attn":
                return s_relu, 2 * H, k[1] * H + k[2] + 1
            if k[0] == "z":
                return s_zact, 2 * T, k[1] * 2 + k[2] + 1
            if k[0] == "logits":
                return (s_slot, 1, 1) if k[1] else (s_lgr, 2, 1)
            return (s_y if k[0] == "out" else s_wh), H, k[1] + 1

        def stage_read(k):
            if k[0] == "z":
                return s_stfree, 2 * T, k[1] * 2 + k[2] + 1
            return s_keep, 2 * T, k[1] * T + k[2] + 1

        def take(eng, u, i, n, names, ring, read):
            s, per, v = read(names[(n - ring) % len(names)])
            if n >= ring:
                eng.wait_ge(s[u], at(i, per, v))
            elif not isinstance(i, int) or i > 0:
                eng.wait_ge(s[u], at(i, per, v - per))

        def hold(eng, s, v):
            eng.wait_ge(s, v)
            eng.sem_inc(s_held, 1)

        RENEW = 12

        def run_graphs(eng, name_of_engine, step):
            def both(u, i_first, i_second):
                for n, (half, name) in enumerate(CYCLE[name_of_engine]):
                    if n % RENEW == 0 and not isinstance(i_first, int):
                        eng.reg_mov(turn_regs[0], i_first)
                        eng.reg_mov(turn_regs[1], i_second)
                        i_first, i_second = (eng.snap(r, min_val=0, max_val=TURNS - 1) for r in turn_regs)
                    step(name, 1 - u if half else u, i_second if half else i_first)
            turn_regs = [eng.alloc_register(n) for n in ("turn_of_first", "turn_of_second")]
            for name in FIRST:
                step(name, 0, 0)
            both(1, 0, 0)
            with eng.Fori(0, TURNS - 1) as i:
                both(0, i + 1, i)
                both(1, i + 1, i + 1)
            for name in SECOND:
                step(name, 1, TURNS - 1)

        class Steps:

            def __init__(self, eng, s, per=0, i=0, base=0):
                self.eng, self.s, self.per, self.i, self.n, self.base = eng, s, per, i, 0, base

            def did(self, ins):
                ins.then_inc(self.s, 1)
                self.n += 1
                return self.n

            def value(self, n=None):
                return at(self.i, self.per, self.base + (self.n if n is None else n))

            def wait(self, n=None):
                self.eng.wait_ge(self.s, self.value(n))

            def hold(self):
                hold(self.eng, self.s, self.value())

            def turn(self, first, i):
                if first:
                    assert self.n in (0, self.per), self.n
                    self.n = 0
                self.i = i

        block = ctx.enter_context(nc.Block())

        DVE_TURN, POOL_TURN = a["dve_turn"], a["pool_turn"]

        @block.sync
        def _(eng):
            eng.dma_start(ident[:, :], a["ident"]).then_inc(s_const, 16)
            eng.dma_start(xr[0][:, 2, 0:P], a["before"]).then_inc(s_const, 16)
            eng.dma_start(cst[:, :], a["cst"]).then_inc(s_const, 16)
            eng.dma_start(nw[:, :], a["nw"]).then_inc(s_const, 16)
            eng.dma_start(rw1[:, :, :], a["rw1"].rearrange("(k p) e -> p k e", p=P)).then_inc(s_const, 16)
            eng.dma_start(w0a[:, :, :], a["a0"].rearrange("(k p) e -> p k e", p=P)).then_inc(s_const, 16)
            eng.dma_start(w1a[:, :, :], a["a1"].rearrange("(k p) e -> p k e", p=P)).then_inc(s_const, 16)
            eng.dma_start(gw1[:, :, :], a["gw1"].rearrange("(k p) e -> p k e", p=P)).then_inc(s_const, 16)
            eng.dma_start(ow[:, :, :], a["ow"].rearrange("(k p) e -> p k e", p=P)).then_inc(s_const, 16)
            eng.dma_start(S[1][:, :, :].rearrange("p (k a) n -> p k (a n)", k=KC), a["ew"].rearrange("(k p) f -> p k f", p=P)).then_inc(s_wld, 16)
            eng.dma_start(xr[0][:, 1, 0:KC * E0].rearrange("p (k e) -> p k e", k=KC), a["rw0"].rearrange("(k p) e -> p k e", p=P)).then_inc(s_wld, 16)
            eng.dma_start(S[0][:, 0, :].rearrange("p (k f) -> p k f", k=KC), a["gw0t"].rearrange("(k p) e -> p k e", p=P)).then_inc(s_wld, 16)
            eng.dma_start(S[0][:, 1, :].rearrange("p (k f) -> p k f", k=KC), a["gw1t"].rearrange("(k p) e -> p k e", p=P)).then_inc(s_wld, 16)
            eng.dma_start(xr[0][:, 0, 0:E1 * 2 * HC], a["fb1"]).then_inc(s_wld, 16)
            eng.dma_start(xr[1][:, 0, 0:BSP], a["brow"]).then_inc(s_wld, 16)
            eng.wait_ge(s_setup, 1)
            for k in range(3):
                eng.dma_start(parts_d[k, :].rearrange("(p b) -> p b", p=P), xn[0][:, k, 0:BSP // 2].bitcast(BF16)[:, 0:BSP]).then_inc(s_bst, 16)
            eng.wait_ge(s_bst, 48)
            eng.dma_start(brow[:, :], parts_d[:, 0:NB0]).then_inc(s_bl, 16)
            eng.wait_ge(s_setup, 2)
            with eng.Fori(0, TURNS) as i:
                def load_graph(u):
                    hold(eng, s_xr[u], at(i, 3 * H, H))
                    eng.dma_start(xin[u][:, :, :], x_v[bass.ds(i * U + u, 1)].rearrange("b p t d -> p (b t) d")).then_inc(s_x[u], 16)
                    hold(eng, s_link[1 - u], at(i, 1, 1))
                    eng.dma_start(adj[:, :, :], adj_v[bass.ds(i * U + u, 1)].rearrange("b p t d -> p (b t) d")).then_inc(s_adj[u], 16)

                def load_fc1(k):
                    hold(eng, s_wsp, at(i, 3, k + 1))
                    eng.dma_start(wst[:, :], f1_v[bass.ds(i, 1), :, k, :].rearrange("e p f -> p (e f)")).then_inc(s_wst, 16)

                load_graph(0)
                load_fc1(0)
                load_graph(1)
                load_fc1(1)
                hold(eng, s_wsp, at(i, 3, 3))
                eng.dma_start(wst[:, :].rearrange("p (k f) -> p k f", k=HC), f2_v[bass.ds(i, 1)].rearrange("e p k f -> p (e k) f")).then_inc(s_wst, 16)
            for u in range(U):
                eng.wait_ge(s_scat[u], 16 + TURNS * 2 * T * 16)
                eng.wait_ge(s_store[u], 16 + TURNS * 16)
            eng.wait_ge(s_table, 1)
            for e in range(E1):
                r = eng.value_load(basei[0:1, e:e + 1], min_val=0, max_val=E1 * REGION)
                eng.dma_start(rows[bass.ds(r, SLOTS), :].rearrange("(s p) d -> p s d", p=P), pad).then_inc(s_padw, 16)
            eng.wait_ge(s_padw, 16 * E1)
            eng.wait_ge(s_add, 48)
            for j in range(2):
                r = eng.value_load(tile_row[0:1, j + 1:j + 2], min_val=0, max_val=E1 * REGION)
                eng.dma_start(gx[j], rows[bass.ds(r, SLOTS), :].rearrange("(s p) d -> p s d", p=P)).then_inc(s_gx[j], 16)
            with eng.Fori(0, TILES // 2) as i:
                for v in range(2):
                    hold(eng, s_sel, at(i, 2, v + 2))
                    hold(eng, s_gtr, at(i, 2, v + 1))
                    r = eng.value_load(tile_row[0:1, bass.ds(i * 2 + v + 3, 1)], min_val=0, max_val=E1 * REGION)
                    eng.dma_start(gx[v], rows[bass.ds(r, SLOTS), :].rearrange("(s p) d -> p s d", p=P)).then_inc(s_gx[v], 16)
            for v in range(2):
                eng.wait_ge(s_gx[v], 16 * (TILES // 2 + 1))
            eng.wait_ge(s_add, 48 + TILES * 2 * 16)

        @block.gpsimd
        def _(eng):
            for s, n in ([(s, XR_FIRST) for s in s_xr] + [(s_link[1], 1), (s_wsp, 1), (s_av, HC), (s_sel, 1)]
                         + [(s, 16) for s in s_store]):
                eng.sem_inc(s, n)
            eng.dma_start(rb0[:, :], a["rb0"]).then_inc(s_scat[0], 16)
            eng.dma_start(rb1[:, :], a["rb1"]).then_inc(s_scat[1], 16)
            eng.memset(mhalf[:, :], -0.5).then_inc(s_gs, 1)
            eng.memset(ones[:, :], 1.0).then_inc(s_gs, 1)
            eng.memset(unscale[:, :], 1.0 / SZ).then_inc(s_gs, 1)
            pst = [Steps(eng, s_pool[u], POOL_TURN[u]) for u in range(U)]

            def step(name, u, i):
                st = pst[u]
                st.turn(name == FIRST[0], i)

                def rsqrt(o, v, cols, scale, eps, ready):
                    st.did(eng.tensor_scalar(ve[:, u, cols], v, scale, eps, ALU.mult, ALU.add))
                    st.wait()
                    eng.tensor_tensor(o, ve[:, u, cols], mhalf[:, cols], ALU.pow).then_inc(ready, 1)

                def split(n, hi, lo):
                    if u:
                        return
                    w = wst[:, :]
                    hold(eng, s_wst, at(i, 48, 16 * (n + 1)))
                    st.did(eng.tensor_scalar(w, w, SW, 0.0, ALU.mult, ALU.add))
                    st.wait()
                    st.did(eng.tensor_copy(hi, w))
                    st.wait()
                    eng.tensor_tensor(lo, w, hi, ALU.subtract).then_inc(s_wsp, 1)

                if name.startswith("stats"):
                    hold(eng, s_var[u], at(i, 4, int(name[-1]) + 1))
                    rsqrt(rstd[:, u, :], mv[:, u, :, 1], slice(0, T), 1.0, LN_EPS, s_rstd[u])
                elif name.startswith("x2"):
                    h = int(name[-1])
                    hold(eng, s_ssq[u], at(i, T, 2 * h + 2))
                    v = slice(2 * h, 2 * h + 2)
                    rsqrt(rr[:, u, v], ss[:, u, v], v, 1.0 / D, RMS_EPS, s_rr[u])
                elif name == "link":
                    hold(eng, s_adj[u], at(i, 16, 16))
                    eng.tensor_scalar(link[u][:, :, :], adj[:, :, :], -NOT_LINKED, NOT_LINKED, ALU.mult, ALU.add).then_inc(s_link[u], 1)
                elif name in ("split0", "split1"):
                    k = int(name[-1])
                    split(k, *(w[:, bass.ds(at(i, 1, 0), 1), k, :].rearrange("p e f -> p (e f)") for w in (f1h, f1l)))
                elif name == "split2":
                    split(2, *(w[:, bass.ds(at(i, 1, 0), 1), :, :].rearrange("p e k f -> p (e k f)") for w in (f2h, f2l)))
                elif name == "send" and (not isinstance(i, int) or i > 0):
                    hold(eng, s_slot[u], at(i, 1, 0))
                    for k in range(2):
                        for t in range(T):
                            eng.indirect_dma_start(rows, bass.IndirectOffsetOnAxis(slot[:, u, k, t:t + 1], 0),
                                                   pay[u][:, t, :], None).then_inc(s_scat[u], 16)

            run_graphs(eng, "gpsimd", step)
            for u in range(U):
                step("send", u, TURNS)
            eng.wait_ge(s_table, 1)
            eng.dma_start(out[TOK:TOK + SLOTS, :].rearrange("(s p) d -> p s d", p=P), pad[:, :, 0:D]).then_inc(s_add, 16)
            eng.dma_start(rows[E1 * REGION:, :].rearrange("(s p) d -> p s d", p=P), pad).then_inc(s_add, 16)
            eng.dma_start(brow2, parts_d[:, NB0:NB]).then_inc(s_add, 16)
            with eng.Fori(0, TILES // 2) as i:
                for v in range(2):
                    hold(eng, s_ys, at(i, 2, v + 1))
                    hold(eng, s_add, at(i, 64, 48 + 32 * v))
                    q = 1 - v
                    for s in range(2):
                        eng.indirect_dma_start(out, bass.IndirectOffsetOnAxis(tsel[:, q, s:s + 1], 0),
                                               ys[q][:, s, :], None, compute_op=ALU.add).then_inc(s_add, 16)

        @block.scalar
        def _(eng):
            def step(name, u, i):
                def filled(k):
                    eng.wait_ge(s_bank[u], at(i, NBANK, BANK_AT[k] + 1))
                    return banks[u][BANK_AT[k] % NB_RING]

                def staging(k):
                    take(eng, u, i, STAGE_AT[k], STAGED, NST, stage_read)
                    return stage[u][STAGE_AT[k] % NST][:, :]

                if name in ("xt0", "xt2", "xt3", "comb"):
                    for h in range(H):
                        b = filled(("comb", h) if name == "comb" else ("xn", int(name[-1]), h))
                        eng.activation(xt[u][:, :, h * 2 * P:(h + 1) * 2 * P], b[:, :].rearrange("p (k n) -> p k n", k=KC),
                                       ACT.Copy).then_inc(s_xt[u], 1)
                elif name == "wh":
                    for h in range(H):
                        b = filled(("wh", h))
                        eng.activation(comb[u][:, 2 * h:2 * h + 2, :].rearrange("p t d -> p (t d)"), b[:, :], ACT.Copy)\
                           .then_inc(s_wh[u], 1)
                elif name.startswith("scores") or name.startswith("keep"):
                    l = int(name[6] if name[0] == "s" else name[4])
                    ahead = NST // (1 + l)
                    if name[0] == "s":
                        eng.wait_ge(s_mxr[u], at(i, 2, l + 1))
                    for t in range(ahead) if name[0] == "s" else [k for k in (int(name[-1]),) if k >= ahead]:
                        eng.activation(staging(("p", l, t, 0)), S[u][:, t, :], ACT.Exp, bias=b1[:, u, t:t + 1]).then_inc(s_p[u], 1)
                        o2 = staging(("p", l, t, 1)) if l else S[u][:, t, :]
                        eng.activation(o2, S[u][:, t, :], ACT.Exp, bias=b2[:, u, t:t + 1], scale=SLOPE).then_inc(s_p[u], 1)
                elif name in ("pt0", "pt1"):
                    for t in range(T):
                        b = filled(("p", int(name[-1]), t))
                        eng.activation(PT[u][:, t, :, :], b[:, :].rearrange("p (k n) -> p k n", k=T), ACT.Copy).then_inc(s_pt[u], 1)
                elif name.startswith("attn"):
                    l, h = int(name[4]), int(name[-1])
                    eng.wait_ge(s_rinv[u], at(i, 2, l + 1))
                    b = filled(("attn", l, h))
                    for t2 in range(2):
                        t = 2 * h + t2
                        eng.activation(SE[u][:, h, 0, t2 * D:(t2 + 1) * D], b[:, t2 * D:(t2 + 1) * D],
                                       ACT.Exp, scale=rinv[:, u, t:t + 1]).then_inc(s_elu[u], 1)
                elif name == "xh1":
                    for h in range(H):
                        b = filled(("xn", 1, h))
                        eng.activation(xh[u][:, 0, :, h * 2 * P:(h + 1) * 2 * P], b[:, :].rearrange("p (k n) -> p k n", k=KC),
                                       ACT.Copy, scale=SX).then_inc(s_xh[u], 1)
                elif name in ("top0", "top1"):
                    eng.wait_ge(s_dif[u], at(i, 2, int(name[-1]) + 1))
                    eng.activation(e2[:, u, :], dif[:, u, :], ACT.Exp).then_inc(s_e2[u], 1)
                elif name[0] == "z":
                    t = int(name[1:])
                    for g in range(2):
                        b = filled(("z", t, g))
                        eng.activation(staging(("z", t, g)), b[:, :], ACT.Tanh, scale=0.5 / SZ).then_inc(s_tanh[u], 1)
                elif name == "y":
                    for h in range(H):
                        eng.wait_ge(s_y[u], at(i, H, h + 1))
                        for t in (2 * h, 2 * h + 1):
                            eng.activation(S[u][:, t, 0:D], comb[u][:, t, :], ACT.Square, accum_out=ss[:, u, t:t + 1]).then_inc(s_ssq[u], 1)
                elif name == "store":
                    eng.wait_ge(s_xr[u], at(i, 3 * H, XR_FIRST + 3 * H))
                    eng.dma_start(out_v[bass.ds(at(i, U, u), 1)].rearrange("b p t d -> p (b t) d"), xr[u][:, :, :]).then_inc(s_store[u], 16)

            run_graphs(eng, "scalar", step)

            eng.wait_ge(s_gtr, 1)
            eng.activation(gxh[0][:, 0, :, :], ptr[0][:, :].rearrange("p (k n) -> p k n", k=KC), ACT.Copy, scale=SX).then_inc(s_gxh, 1)
            with eng.Fori(0, TILES // 2) as i:
                for v in range(2):
                    q = 1 - v
                    eng.wait_ge(s_bsel, at(i, 2, v + 1))
                    for c in range(HC):
                        eng.wait_ge(s_h, at(i, 2 * HC, v * HC + c + 1))
                        eng.activation(th[c], pmm[c][:, 0:SLOTS], ACT.Tanh, scale=0.5 / SZ, bias=bsel[:, v, c:c + 1]).then_inc(s_th, 1)
                        eng.activation(z1[c], pmm[c][:, 0:SLOTS], ACT.Identity, scale=0.5 / SZ * SX / SZ,
                                       bias=bsel[:, v, HC + c:HC + c + 1]).then_inc(s_th, 1)
                        if c >= 1:
                            eng.wait_ge(s_av, at(i, 2 * HC, HC + v * HC + c))
                            eng.activation(ah[v][:, c - 1, :], av[c - 1], ACT.Copy).then_inc(s_ah, 1)
                    eng.wait_ge(s_gtr, at(i, 2, v + 2))
                    eng.activation(gxh[q][:, 0, :, :], ptr[q][:, :].rearrange("p (k n) -> p k n", k=KC), ACT.Copy, scale=SX).then_inc(s_gxh, 1)
                    eng.wait_ge(s_av, at(i, 2 * HC, HC + v * HC + HC))
                    eng.activation(ah[v][:, HC - 1, :], av[HC - 1], ACT.Copy).then_inc(s_ah, 1)
                    eng.wait_ge(s_yp, at(i, 2, v + 1))
                    eng.wait_ge(s_add, at(i, 64, 16 + 32 * v))
                    eng.wait_ge(s_sel, at(i, 2, v + 1))
                    for s in range(2):
                        ins = eng.activation(ys[q][:, s, :], (pf if q else psm)[:, s * D:(s + 1) * D], ACT.Copy, scale=gsel[:, q, s:s + 1])
                    ins.then_inc(s_ys, 1)

        @block.tensor
        def _(eng):
            eng.wait_ge(s_const, 16 * 9)
            eng.wait_ge(s_wld, 16 * 6)
            for l, wa in ((0, w0a), (1, w1a)):
                for m in range(KC):
                    for k in range(KC):
                        ins = eng.matmul(psm[:, 4 * l + 2 * m:4 * l + 2 * m + 2],
                                         S[0][:, l, k * D + m * P:k * D + (m + 1) * P], wa[:, k, :],
                                         start=(k == 0), stop=(k == KC - 1))
            ins.then_inc(s_up, 1)
            eng.wait_ge(s_setup, 2)
            eng.wait_ge(s_bl, 16)
            eng.wait_ge(s_gs, 3)

            def step(name, u, i):
                def bank_for(k):
                    n = BANK_AT[k]
                    take(eng, u, i, n, BANKS, NB_RING, bank_read)
                    return banks[u][n % NB_RING]

                def turn_rows(k, h, x):
                    o = bank_for(k)
                    for c in range(KC):
                        for t2 in range(2):
                            ins = eng.transpose(o[:, c * 2 * P + t2 * P:c * 2 * P + (t2 + 1) * P],
                                                x[:, 2 * h + t2, c * P:(c + 1) * P], ident[:, :])
                    ins.then_inc(s_bank[u], 1)

                def xt_at(use):
                    eng.wait_ge(s_xt[u], at(i, 4 * H, (use + 1) * H))

                if name in ("xn0", "xn1", "xn2", "xn3"):
                    j = int(name[-1])
                    for h in range(H):
                        eng.wait_ge(s_xn[u], at(i, 4 * T, j * T + 2 * h + 2))
                        turn_rows(("xn", j, h), h, pay[u] if j == 3 else xn[u])
                elif name in ("f0", "f1"):
                    l = int(name[-1])
                    xt_at(2 * l)
                    o = bank_for(("src", l))
                    for t in range(T):
                        for c in range(KC):
                            ins = eng.matmul(o[:, t:t + 1], xt[u][:, c, t * P:(t + 1) * P], u_src[:, l, c, :],
                                             start=(c == 0), stop=(c == KC - 1))
                    ins.then_inc(s_bank[u], 1)
                    o = bank_for(("f", l))
                    for c in range(KC):
                        ins = eng.matmul(o[:, :], u_dst[:, l, c, :], xt[u][:, c, :], start=(c == 0), stop=(c == KC - 1))
                    ins.then_inc(s_bank[u], 1)
                elif name == "wh":
                    for h in range(H):
                        o = bank_for(("wh", h))
                        for t2 in range(2):
                            t = 2 * h + t2
                            for c in range(KC):
                                ins = eng.matmul(o[:, t2 * D:(t2 + 1) * D], xt[u][:, c, t * P:(t + 1) * P], gw1[:, c, :],
                                                 start=(c == 0), stop=(c == KC - 1))
                        ins.then_inc(s_bank[u], 1)
                elif name.startswith("keep"):
                    l, t = int(name[4]), int(name[-1])
                    eng.wait_ge(s_keep[u], at(i, 2 * T, l * T + t + 1))
                    o = bank_for(("p", l, t))
                    for m in range(T):
                        ins = eng.transpose(o[:, m * P:(m + 1) * P], S[u][:, t, m * P:(m + 1) * P], ident[:, :])
                    ins.then_inc(s_bank[u], 1)
                elif name.startswith("attn"):
                    l, h = int(name[4]), int(name[-1])
                    if l and h == 0:
                        eng.wait_ge(s_wh[u], at(i, H, H))
                    val = comb[u] if l else xn[u]
                    eng.wait_ge(s_pt[u], at(i, 2 * T, l * T + 2 * h + 2))
                    o = banks[u][BANK_AT[("attn", l, h)] % NB_RING]
                    for t2 in range(2):
                        for m in range(T):
                            ins = eng.matmul(o[:, t2 * D:(t2 + 1) * D], PT[u][:, 2 * h + t2, m, :], val[:, m, :],
                                             start=(m == 0), stop=(m == T - 1))
                    ins.then_inc(s_bank[u], 1)
                elif name == "logits0":
                    eng.wait_ge(s_xl[u], at(i, H, H))
                    o = bank_for(("logits", 0))
                    for t in range(T):
                        n = 0
                        for c in range(KC):
                            for s, w in ((0, rwh), (1, rwh), (0, rwl)):
                                ins = eng.matmul(o[:, t * E0:(t + 1) * E0], xh[u][:, s, c, t * P:(t + 1) * P], w[:, c, :],
                                                 start=(n == 0), stop=(n == 5))
                                n += 1
                    ins.then_inc(s_bank[u], 1)
                elif name[0] == "z":
                    t = int(name[1:])
                    for g in range(2):
                        o = bank_for(("z", t, g))
                        eng.matmul(o[:, :], ones[0:3, :], brow[:, g * BANK:(g + 1) * BANK], start=True, stop=False)
                        for c in range(KC):
                            for s, w in ((0, ewh), (0, ewl), (1, ewh)):
                                ins = eng.matmul(o[:, :], xh[u][:, s, c, t * P:(t + 1) * P], w[:, c, g * BANK:(g + 1) * BANK],
                                                 start=False, stop=(c == KC - 1 and s == 1))
                        ins.then_inc(s_bank[u], 1)
                elif name == "comb":
                    for h in range(H):
                        eng.wait_ge(s_stfree[u], at(i, 2 * T, (2 * h + 2) * 2))
                        turn_rows(("comb", h), h, comb[u])
                elif name == "out":
                    xt_at(1)
                    for h in range(H):
                        o = bank_for(("out", h))
                        for t2 in range(2):
                            t = 2 * h + t2
                            eng.matmul(o[:, t2 * D:(t2 + 1) * D], unscale[:, :], brow[:, E0 * D:E0 * D + D], start=True, stop=False)
                            for c in range(KC):
                                ins = eng.matmul(o[:, t2 * D:(t2 + 1) * D], xt[u][:, c, t * P:(t + 1) * P], ow[:, c, :],
                                                 start=False, stop=(c == KC - 1))
                        ins.then_inc(s_bank[u], 1)
                elif name == "logits1":
                    xt_at(3)
                    o = bank_for(("logits", 1))
                    for t in range(T):
                        for c in range(KC):
                            ins = eng.matmul(o[:, t * E1:(t + 1) * E1], xt[u][:, c, t * P:(t + 1) * P], rw1[:, c, :],
                                             start=(c == 0), stop=(c == KC - 1))
                    ins.then_inc(s_bank[u], 1)
                elif name == "choice":
                    o = banks[u][BANK_AT[("logits", 1)] % NB_RING]
                    eng.wait_ge(s_chose[u], at(i, 1, 1))
                    for t in range(T):
                        for t1 in range(t + 1):
                            eng.matmul(o[:, POS.start + t * E1:POS.start + (t + 1) * E1], before[:, :] if t1 == t else ones[:, :],
                                       chose[:, u, t1, :], start=(t1 == 0), stop=(t1 == t))
                    for t in range(T):
                        ins = eng.matmul(o[:, TOT], ones[:, :], chose[:, u, t, :], start=(t == 0), stop=(t == T - 1))
                    ins.then_inc(s_pos[u], 1)

            run_graphs(eng, "tensor", step)

            def turn_tile(v):
                for c in range(KC):
                    for s in range(2):
                        ins = eng.transpose(ptr[v][:, c * SLOTS + s * P:c * SLOTS + (s + 1) * P],
                                            gx[v][:, s, c * P:(c + 1) * P], ident[:, :])
                ins.then_inc(s_gtr, 1)

            eng.wait_ge(s_gx[0], 16)
            turn_tile(0)
            eng.wait_ge(s_wsp, 1 + 3 * TURNS)
            eng.wait_ge(s_add, 48)
            eng.wait_ge(s_table, 2)
            with eng.Fori(0, TILES // 2) as i:
                for v in range(2):
                    q = 1 - v
                    e = eng.value_load(tile_expert[0:1, bass.ds(i * 2 + v + 1, 1)], min_val=0, max_val=E1 - 1)
                    eng.wait_ge(s_gxl, at(i, 2, v + 1))
                    for c in range(HC):
                        eng.wait_ge(s_av, at(i, 2 * HC, v * HC + c + 1))
                        for half in range(2):
                            n = 0
                            for k in range(KC):
                                f = half * HID + c * P
                                for w, s in ((f1h, 0), (f1h, 1), (f1l, 0)):
                                    ins = eng.matmul(pmm[c][:, half * SLOTS:(half + 1) * SLOTS],
                                                     w[:, bass.ds(e, 1), k, f:f + P].rearrange("p e f -> p (e f)"),
                                                     gxh[v][:, s, k, :], start=(n == 0), stop=(n == 5))
                                    n += 1
                        ins.then_inc(s_h, 1)
                    eng.wait_ge(s_gx[q], at(i, 16, 16 + 16 * v))
                    turn_tile(q)
                    hold(eng, s_al, at(i, 2 * HC, v * HC + 1))
                    e = eng.value_load(tile_expert[0:1, bass.ds(i * 2 + v, 1)], min_val=0, max_val=E1 - 1)
                    y = pf if q else psm
                    for s in range(2):
                        o = y[:, s * D:(s + 1) * D]
                        eng.matmul(o, ones[0:3, :], brow2[:, bass.ds(e * D, D)], start=True, stop=False)
                        for c in range(HC):
                            for x, w in ((ah, f2h), (ah, f2l), (al, f2h)):
                                ins = eng.matmul(o, x[q][:, c, s * P:(s + 1) * P],
                                                 w[:, bass.ds(e, 1), c, :].rearrange("p e f -> p (e f)"),
                                                 start=False, stop=(c == HC - 1 and x is al))
                    ins.then_inc(s_yp, 1)

        @block.vector
        def _(eng):
            st = Steps(eng, s_dve[U])
            did, wait = st.did, st.wait
            eng.wait_ge(s_wld, 16 * 6)
            eng.wait_ge(s_const, 16 * 9)
            b, r1, r2 = (xr[1][:, k, 0:BSP] for k in range(3))
            parts = [xn[0][:, k, 0:BSP // 2].bitcast(BF16)[:, 0:BSP] for k in range(3)]
            did(eng.tensor_scalar(b, b, SZ, 0.0, ALU.mult, ALU.add))
            wait()
            did(eng.tensor_copy(parts[0], b))
            wait()
            did(eng.tensor_tensor(r1, b, parts[0], ALU.subtract))
            wait()
            did(eng.tensor_copy(parts[1], r1))
            wait()
            did(eng.tensor_tensor(r2, r1, parts[1], ALU.subtract))
            wait()
            eng.tensor_copy(parts[2], r2).then_inc(s_setup, 1)
            did(eng.tensor_copy(before[:, :], xr[0][:, 2, 0:P]))
            did(eng.memset(lg[:, :, :, :], NOT_LINKED))
            did(eng.tensor_copy(base[:, :], ebase))
            did(eng.tensor_copy(tokf[:, 0, :], tok0))
            did(eng.tensor_scalar(tokf[:, 1, :], tok0, float(N), 0.0, ALU.add, ALU.add))
            for w, hi, lo in ((S[1][:, :, :].rearrange("p a n -> p (a n)"), ewh[:, :, :].rearrange("p k f -> p (k f)"), ewl[:, :, :].rearrange("p k f -> p (k f)")),
                              (xr[0][:, 1, 0:KC * E0], rwh[:, :, :].rearrange("p k f -> p (k f)"), rwl[:, :, :].rearrange("p k f -> p (k f)"))):
                did(eng.tensor_scalar(hi, w, SW, 0.0, ALU.mult, ALU.add))
                wait()
                did(eng.scalar_tensor_tensor(lo, w, SW, hi, ALU.mult, ALU.subtract))
            for k in range(U):
                eng.wait_ge(s_scat[k], 16)
            fbv = xr[0][:, 0, 0:E1 * 2 * HC].rearrange("p (e c) -> p e c", e=E1)
            did(eng.tensor_scalar(fb[:, :, 0:HC], fbv[:, :, 0:HC], 0.5, 0.0, ALU.mult, ALU.add))
            did(eng.tensor_scalar(fb[:, :, HC:2 * HC], fbv[:, :, 0:HC], 0.5 * SX / SZ, 0.0, ALU.mult, ALU.add))
            did(eng.tensor_scalar(fb[:, :, 2 * HC:3 * HC], fbv[:, :, HC:2 * HC], SZ, 0.0, ALU.mult, ALU.add))
            eng.wait_ge(s_up, 1)
            for l in range(2):
                for k in range(KC):
                    did(eng.tensor_copy(u_src[:, l, k, :], psm[:, 4 * l + 2 * k:4 * l + 2 * k + 1]))
                    did(eng.tensor_copy(u_dst[:, l, k, :], psm[:, 4 * l + 2 * k + 1:4 * l + 2 * k + 2].to_broadcast([P, P])))
            wait()
            eng.memset(zero8[:, :], 0.0).then_inc(s_setup, 1)
            DVE_SETUP = st.n
            eng.wait_ge(s_setup, 2)

            dst = [Steps(eng, s_dve[u], DVE_TURN) for u in range(U)]

            def step(name, u, i):
                st = dst[u]
                st.turn(name == FIRST[0], i)
                did, wait = st.did, st.wait

                def bc(x, n):
                    return x.unsqueeze(2).to_broadcast([P, T, n])

                def filled(k):
                    eng.wait_ge(s_bank[u], at(i, NBANK, BANK_AT[k] + 1))
                    return banks[u][BANK_AT[k] % NB_RING]

                def staged(k):
                    return stage[u][STAGE_AT[k] % NST]

                def half_stats(x, h):
                    for t in (2 * h, 2 * h + 1):
                        did(eng.bn_stats(stats[:, u, t, :], x[:, t, :]))

                def gates(j):
                    hold(eng, s_lgr[u], at(i, 2, j + 1))
                    for t in range(T):
                        did(eng.max(m8[:, u, t, :], lg[:, u, t, :]))
                    st.hold()
                    for t in range(T):
                        did(eng.max_index(i8[:, u, t, :], m8[:, u, t, :], lg[:, u, t, :]))
                    eng.tensor_tensor(dif[:, u, :], m8[:, u, :, 1], m8[:, u, :, 0], ALU.subtract).then_inc(s_dif[u], 1)
                    wait()
                    did(eng.tensor_copy(i8f[:, u, :, :], i8[:, u, :, 0:2]))
                    wait()
                    it = iota8.unsqueeze(1).to_broadcast([P, T, 8])
                    did(eng.tensor_tensor(oh1[:, u, :, :], it, bc(i8f[:, u, :, 0], 8), ALU.is_equal))
                    did(eng.tensor_tensor(oh2[:, u, :, :], it, bc(i8f[:, u, :, 1], 8), ALU.is_equal))

                def gates_end(j, gate, scale):
                    eng.wait_ge(s_e2[u], at(i, 2, j + 1))
                    did(eng.tensor_scalar(den[:, u, :], e2[:, u, :], 1.0 / scale, 1.0 / scale, ALU.mult, ALU.add))
                    wait()
                    did(eng.reciprocal(w1[:, u, :], den[:, u, :]))
                    wait()
                    did(eng.tensor_tensor(w2[:, u, :], e2[:, u, :], w1[:, u, :], ALU.mult))
                    did(eng.tensor_tensor(g1[:, u, :, :], oh1[:, u, :, :], bc(w1[:, u, :], 8), ALU.mult))
                    wait()
                    did(eng.tensor_tensor(g2[:, u, :, :], oh2[:, u, :, :], bc(w2[:, u, :], 8), ALU.mult))
                    wait()
                    did(eng.tensor_tensor(gate, g1[:, u, :, :], g2[:, u, :, :], ALU.add))

                if name.startswith("stats"):
                    j = int(name[-1])
                    if j == 0:
                        eng.wait_ge(s_x[u], at(i, 16, 16))
                        for h in range(H):
                            half_stats(xin[u], h)
                    st.hold()
                    for t in range(T):
                        ins = eng.bn_aggr(mv[:, u, t, :], stats[:, u, t, :])
                    ins.then_inc(s_var[u], 1)
                elif name.startswith("xn"):
                    j = int(name[-1])
                    x = xr[u] if j else xin[u]
                    o = pay[u] if j == 3 else xn[u]
                    eng.wait_ge(s_rstd[u], at(i, 4, j + 1))
                    if j == 3:
                        eng.wait_ge(s_scat[u], at(i, 2 * T * 16, 16))
                    for t in range(T):
                        eng.tensor_scalar(o[:, t, 0:D], x[:, t, :], mv[:, u, t, 0:1], rstd[:, u, t:t + 1],
                                          ALU.subtract, ALU.mult).then_inc(s_xn[u], 1)
                elif name in ("scores0", "scores1"):
                    l = int(name[-1])
                    if l == 0:
                        eng.wait_ge(s_link[u], at(i, 1, 1 + u))
                    b = filled(("src", l))
                    did(eng.tensor_copy(src[:, u, :], b[:, 0:T]))
                    hold(eng, s_bank[u], at(i, NBANK, BANK_AT[("f", l)] + 1))
                    b = banks[u][BANK_AT[("f", l)] % NB_RING]
                    for t in range(T):
                        eng.tensor_tensor_reduce(out=S[u][:, t, :], in0=b[:, :], in1=link[u][:, t, :], scale=1.0,
                                                 scalar=4 * NOT_LINKED, op0=ALU.add, op1=ALU.max,
                                                 accum_out=mrow[:, u, t:t + 1]).then_inc(s_sc[u], 1)
                    eng.wait_ge(s_sc[u], at(i, 2 * T, (l + 1) * T))
                    wait()
                    did(eng.tensor_tensor(mrow[:, u, :], mrow[:, u, :], src[:, u, :], ALU.add))
                    wait()
                    did(eng.scalar_tensor_tensor(mx[:, u, :], mrow[:, u, :], SLOPE, mrow[:, u, :], ALU.mult, ALU.max))
                    wait()
                    did(eng.tensor_tensor(b1[:, u, :], src[:, u, :], mx[:, u, :], ALU.subtract))
                    eng.scalar_tensor_tensor(b2[:, u, :], src[:, u, :], SLOPE, mx[:, u, :], ALU.mult, ALU.subtract).then_inc(s_mxr[u], 1)
                elif name.startswith("kth"):
                    h = int(name[3:])
                    rest = xn[u][:, :, :].rearrange("p (two a) b -> p two (a b)", two=2)
                    for t in (2 * h, 2 * h + 1):
                        did(eng.max(top[:, u, t, :], S[u][:, t, :]))
                    st.hold()
                    for t in (2 * h, 2 * h + 1):
                        did(eng.match_replace(rest[:, t % 2, :], top[:, u, t, :], S[u][:, t, :], 2 * NOT_LINKED))
                    st.hold()
                    for t in (2 * h, 2 * h + 1):
                        did(eng.max(top2[:, u, t, :], rest[:, t % 2, :]))
                elif name.startswith("keep"):
                    l, t = int(name[4]), int(name[-1])
                    eng.wait_ge(s_p[u], at(i, 4 * T, (l * T + t + 1) * 2))
                    s, q = S[u][:, t, :], staged(("p", l, t, 0))[:, :]
                    if l == 0:
                        eng.scalar_tensor_tensor(s, q, 1.0, s, ALU.mult, ALU.max, accum_out=rs[:, u, t:t + 1]).then_inc(s_keep[u], 1)
                    else:
                        did(eng.scalar_tensor_tensor(q, q, 1.0, staged(("p", l, t, 1))[:, :], ALU.mult, ALU.max,
                                                     accum_out=rs[:, u, t:t + 1]))
                        wait()
                        eng.scalar_tensor_tensor(s, s, top2[:, u, t, 7:8], q, ALU.is_ge, ALU.mult).then_inc(s_keep[u], 1)
                    if t == T - 1:
                        eng.wait_ge(s_keep[u], at(i, 2 * T, (l + 1) * T))
                        eng.reciprocal(rinv[:, u, :], rs[:, u, :]).then_inc(s_rinv[u], 1)
                elif name.startswith("elu"):
                    l, h = int(name[3]), int(name[-1])
                    if h == 0:
                        eng.wait_ge(s_rinv[u], at(i, 2, l + 1))
                    b = banks[u][BANK_AT[("attn", l, h)] % NB_RING]
                    eng.wait_ge(s_elu[u], at(i, 2 * T, l * T + 2 * h + 2))
                    r = SE[u][:, h, 1, :]
                    for t2 in range(2):
                        ins = eng.tensor_scalar(r[:, t2 * D:(t2 + 1) * D], b[:, t2 * D:(t2 + 1) * D],
                                                rinv[:, u, 2 * h + t2:2 * h + t2 + 1], 0.0, ALU.mult, ALU.max)
                    ins.then_inc(s_relu[u], 1)
                    eng.wait_ge(s_relu[u], at(i, 2 * H, l * H + h + 1))
                    did(eng.scalar_tensor_tensor(r, SE[u][:, h, 0, :], 1.0, r, ALU.min, ALU.add))
                    wait()
                    if l == 0:
                        eng.wait_ge(s_store[u], at(i, 16, 16))
                    o = xr[u][:, 2 * h:2 * h + 2, :].rearrange("p t d -> p (t d)")
                    x = (xr[u] if l else xin[u])[:, 2 * h:2 * h + 2, :].rearrange("p t d -> p (t d)")
                    eng.scalar_tensor_tensor(o, r, -1.0, x, ALU.add, ALU.add).then_inc(s_xr[u], 1)
                    eng.wait_ge(s_xr[u], at(i, 3 * H, XR_FIRST + 2 * l * H + h + 1))
                    half_stats(xr[u], h)
                elif name == "xl1":
                    for h in range(H):
                        eng.wait_ge(s_xh[u], at(i, H, h + 1))
                        n = slice(h * 2 * P, (h + 1) * 2 * P)
                        b = banks[u][BANK_AT[("xn", 1, h)] % NB_RING]
                        eng.scalar_tensor_tensor(xh[u][:, 1, :, n], b[:, :].rearrange("p (k n) -> p k n", k=KC), SX,
                                                 xh[u][:, 0, :, n], ALU.mult, ALU.subtract).then_inc(s_xl[u], 1)
                elif name == "logits0":
                    wait()
                    did(eng.memset(lg[:, u, :, E0:8], NOT_LINKED))
                    b = filled(("logits", 0))
                    eng.scalar_tensor_tensor(lg[:, u, :, 0:E0], b[:, 0:T * E0].rearrange("p (t e) -> p t e", t=T), 1.0 / SZ,
                                             rb0[:, :].unsqueeze(1).to_broadcast([P, T, E0]), ALU.mult, ALU.add).then_inc(s_lgr[u], 1)
                    wait()
                    gates(0)
                elif name == "top0":
                    gates_end(0, gate0[:, u, :, :], 0.5 / SZ)
                elif name[0] == "z":
                    t = int(name[1:])
                    for g in range(2):
                        z = staged(("z", t, g))
                        n = t * 2 + g + 1
                        b = banks[u][BANK_AT[("z", t, g)] % NB_RING]
                        eng.wait_ge(s_tanh[u], at(i, 2 * T, n))
                        eng.scalar_tensor_tensor(z[:, :], z[:, :], 1.0, b[:, :], ALU.add, ALU.mult).then_inc(s_zact[u], 1)
                        eng.wait_ge(s_zact[u], at(i, 2 * T, n))
                        if n == 1:
                            wait()
                        for e in range(2):
                            ex = 2 * g + e
                            gt = gate0[:, u, t, ex:ex + 1]
                            o = comb[u][:, t, :]
                            if ex == 0:
                                ins = eng.tensor_scalar(o, z[:, e * D:(e + 1) * D], gt, 0.0, ALU.mult, ALU.add)
                            else:
                                ins = eng.scalar_tensor_tensor(o, z[:, e * D:(e + 1) * D], gt, o, ALU.mult, ALU.add)
                            if e == 1:
                                ins.then_inc(s_stfree[u], 1)
                                if g == 0:
                                    eng.wait_ge(s_stfree[u], at(i, 2 * T, n))
                            else:
                                did(ins)
                                wait()
                elif name == "y":
                    for h in range(H):
                        b = filled(("out", h))
                        v = slice(2 * h, 2 * h + 2)
                        eng.tensor_tensor(comb[u][:, v, :].rearrange("p t d -> p (t d)"), b[:, :],
                                          xn[u][:, v, :].rearrange("p t d -> p (t d)"), ALU.add).then_inc(s_y[u], 1)
                elif name.startswith("x2"):
                    h = int(name[-1])
                    v = slice(2 * h, 2 * h + 2)
                    eng.wait_ge(s_rr[u], at(i, H, h + 1))
                    for t in (2 * h, 2 * h + 1):
                        did(eng.scalar_tensor_tensor(comb[u][:, t, :], comb[u][:, t, :], rr[:, u, t:t + 1], nw[:, :], ALU.mult, ALU.mult))
                    wait()
                    eng.tensor_tensor(xr[u][:, v, :], xr[u][:, v, :], comb[u][:, v, :], ALU.add).then_inc(s_xr[u], 1)
                    eng.wait_ge(s_xr[u], at(i, 3 * H, XR_FIRST + H + h + 1))
                    half_stats(xr[u], h)
                elif name == "logits1":
                    b = filled(("logits", 1))
                    eng.tensor_tensor(lg[:, u, :, :], b[:, 0:T * E1].rearrange("p (t e) -> p t e", t=T),
                                      rb1[:, :].unsqueeze(1).to_broadcast([P, T, E1]), ALU.add).then_inc(s_lgr[u], 1)
                    gates(1)
                    wait()
                    eng.tensor_tensor(chose[:, u, :, :], oh1[:, u, :, :], oh2[:, u, :, :], ALU.add).then_inc(s_chose[u], 1)
                elif name == "top1":
                    gates_end(1, pay[u][:, :, D:D + E1], 1.0 / SZ)
                    did(eng.tensor_copy(pay[u][:, :, ROW - 1:ROW].rearrange("p t o -> p (t o)").bitcast(I32), tokf[:, u, :]))
                elif name == "slots":
                    b = banks[u][BANK_AT[("logits", 1)] % NB_RING]
                    eng.wait_ge(s_pos[u], at(i, 1, 1))
                    if u or not isinstance(i, int):
                        eng.wait_ge(s_base, at(i, U, u))
                    did(eng.tensor_tensor(place[:, u, :, :], b[:, POS].rearrange("p (t e) -> p t e", t=T),
                                          base[:, :].unsqueeze(1).to_broadcast([P, T, E1]), ALU.add))
                    wait()
                    did(eng.tensor_tensor(g1[:, u, :, :], place[:, u, :, :], oh1[:, u, :, :], ALU.mult))
                    did(eng.tensor_tensor(g2[:, u, :, :], place[:, u, :, :], oh2[:, u, :, :], ALU.mult))
                    eng.tensor_tensor(base[:, :], b[:, TOT], base[:, :], ALU.add).then_inc(s_base, 1)
                    did(eng.tensor_scalar(tokf[:, u, :], tokf[:, u, :], float(U * N), 0.0, ALU.add, ALU.add))
                    wait()
                    did(eng.tensor_reduce(slotf[:, u, 0, :], g1[:, u, :, :], AX.X, ALU.add))
                    did(eng.tensor_reduce(slotf[:, u, 1, :], g2[:, u, :, :], AX.X, ALU.add))
                    eng.wait_ge(s_base, at(i, U, u + 1))
                    wait()
                    eng.tensor_copy(slot[:, u, :, :], slotf[:, u, :, :]).then_inc(s_slot[u], 1)

            run_graphs(eng, "vector", step)
            assert dst[0].n == dst[1].n == DVE_TURN, dst[0].n

            st = Steps(eng, s_dve[U], base=DVE_SETUP)
            eng.wait_ge(s_base, B)
            did, wait = st.did, st.wait
            did(eng.memset(pad, 0.0))
            did(eng.tensor_copy(basei[:, :], base[0:1, :]))
            did(eng.tensor_tensor(tilesf[:, :], base[0:1, :], ebase[0:1, :], ALU.subtract))
            wait()
            did(eng.tensor_scalar(tilesf[:, :], tilesf[:, :], float(SLOTS - 1), 0.0, ALU.add, ALU.add))
            wait()
            did(eng.tensor_copy(pad[:, :, ROW - 1:ROW].rearrange("p s o -> p (s o)").bitcast(I32), padtok))
            did(eng.tensor_copy(cnti[:, :], tilesf[:, :]))
            wait()
            did(eng.tensor_scalar(cnti[:, :], cnti[:, :], SLOTS.bit_length() - 1, None, ALU.arith_shift_right))
            wait()
            did(eng.tensor_copy(tilesf[:, :], cnti[:, :]))
            wait()
            did(eng.tensor_tensor_scan(tcum[:, :], tilesf[:, :], zero8[:, :], 0.0, ALU.add, ALU.add))
            did(eng.memset(tex, 0.0))
            did(eng.memset(tst, 0.0))
            wait()
            for e in range(E1):
                did(eng.tensor_scalar(tge, jnum, tcum[:, e:e + 1], tilesf[:, e:e + 1], ALU.is_ge, ALU.mult))
                did(eng.scalar_tensor_tensor(tex, jnum, tcum[:, e:e + 1], tex, ALU.is_ge, ALU.add))
                wait()
                did(eng.tensor_tensor(tst, tst, tge, ALU.add))
                wait()
            did(eng.tensor_tensor(tst, jnum, tst, ALU.subtract))
            did(eng.tensor_scalar(tge, tex, float(REGION), 0.0, ALU.mult, ALU.add))
            wait()
            did(eng.scalar_tensor_tensor(tst, tst, float(SLOTS), tge, ALU.mult, ALU.add))
            wait()
            did(eng.tensor_scalar(tst, tst, float(E1 * REGION), 0.0, ALU.min, ALU.max))
            did(eng.tensor_scalar(tex, tex, float(E1 - 1), 0.0, ALU.min, ALU.max))
            wait()
            did(eng.tensor_copy(tile_row[:, :], tst))
            wait()
            eng.tensor_copy(tile_expert[:, :], tex).then_inc(s_table, 1)
            did(eng.memset(ah[1], 0.0))
            did(eng.memset(al[1], 0.0))
            did(eng.memset(gsel[:, 1, :], 0.0))
            did(eng.tensor_copy(tsel[:, 1, :], padtok))
            wait()
            eng.nop().then_inc(s_table, 1)
            eng.wait_ge(s_table, 2)
            eng.sem_inc(s_al, 1)

            def lo(v):
                eng.scalar_tensor_tensor(gxh[v][:, 1, :, :], ptr[v][:, :].rearrange("p (k n) -> p k n", k=KC), SX,
                                         gxh[v][:, 0, :, :], ALU.mult, ALU.subtract).then_inc(s_gxl, 1)
            eng.wait_ge(s_gxh, 1)
            lo(0)
            with eng.Fori(0, TILES // 2) as i:
                for v in range(2):
                    q = 1 - v
                    e = eng.value_load(tile_expert[0:1, bass.ds(i * 2 + v + 1, 1)], min_val=0, max_val=E1 - 1)
                    eng.tensor_copy(bsel[:, v, :], fb[:, bass.ds(e, 1), :].rearrange("p e c -> p (e c)")).then_inc(s_bsel, 1)
                    eng.wait_ge(s_bsel, at(i, 2, v + 1))
                    for c in range(HC):
                        eng.wait_ge(s_th, at(i, 4 * HC, (v * HC + c + 1) * 2))
                        eng.scalar_tensor_tensor(th[c], th[c], 1.0, z1[c], ALU.add, ALU.mult).then_inc(s_silu, 1)
                        eng.wait_ge(s_silu, at(i, 2 * HC, v * HC + c + 1))
                        eng.scalar_tensor_tensor(av[c], pmm[c][:, SLOTS:2 * SLOTS], bsel[:, v, 2 * HC + c:2 * HC + c + 1], th[c],
                                                 ALU.add, ALU.mult).then_inc(s_av, 1)
                        if c >= 1:
                            eng.wait_ge(s_ah, at(i, 2 * HC, v * HC + c))
                            eng.tensor_tensor(al[v][:, c - 1, :], av[c - 1], ah[v][:, c - 1, :], ALU.subtract).then_inc(s_al, 1)
                    eng.wait_ge(s_gxh, at(i, 2, v + 2))
                    lo(q)
                    eng.wait_ge(s_ah, at(i, 2 * HC, v * HC + HC))
                    eng.tensor_tensor(al[v][:, HC - 1, :], av[HC - 1], ah[v][:, HC - 1, :], ALU.subtract).then_inc(s_al, 1)
                    eng.wait_ge(s_gx[v], at(i, 16, 16))
                    eng.wait_ge(s_add, at(i, 64, 48 + 32 * v))
                    eng.tensor_copy(tsel[:, v, :], gx[v][:, :, ROW - 1:ROW].rearrange("p s o -> p (s o)").bitcast(I32))
                    eng.tensor_copy(gsel[:, v, :], gx[v][:, :, bass.ds(e + D, 1)].rearrange("p s o -> p (s o)")).then_inc(s_sel, 1)



def kernel(**inputs):
    import concourse.bacc as bacc
    from concourse.bass_utils import run_bass_kernel_spmd

    f = {k: np.ascontiguousarray(v) for k, v in inputs.items()}

    def rep(v):
        return np.ascontiguousarray(np.broadcast_to(v.reshape(1, -1), (P, v.size)))

    cst = np.zeros((P, 22 + TABLE), np.float32)
    cst[:, 0:8] = np.arange(8)
    cst[:, 8:8 + T] = np.arange(P)[:, None] + P * np.arange(T)
    cst[:, 12:20] = REGION * np.arange(E1)
    cst[:, 20:22] = TOK + np.arange(P)[:, None] + P * np.arange(2)
    cst[:, 22:] = np.arange(TABLE) - 1
    arrays = {
        "x": f["x"].reshape(TOK, D),
        "adj": f["adj"].reshape(TOK, N),
        "ident": np.eye(P, dtype=np.float32),
        "before": np.triu(np.ones((P, P), np.float32), 1),
        "cst": cst,
        "nw": rep(f["L0_ffn_norm_w"]),
        "rb0": rep(f["L0_ffn_router_b"]),
        "rb1": rep(f["L1_ffn_router_b"]),
        "rw0": f["L0_ffn_router_w"],
        "rw1": np.ascontiguousarray(f["L1_ffn_router_w"].T),
        "a0": np.concatenate([f["L0_gnn_a1"], f["L0_gnn_a2"]], 1),
        "a1": np.ascontiguousarray(f["L1_gnn_a"].reshape(2, D).T),
        "gw0t": f["L0_gnn_W"],
        "gw1t": np.ascontiguousarray(f["L1_gnn_W"].T),
        "gw1": f["L1_gnn_W"],
        "ow": f["L0_ffn_out_w"],
        "ew": np.ascontiguousarray(f["L0_ffn_expert_w"].transpose(1, 0, 2)).reshape(D, E0 * D),
        "fb1": np.ascontiguousarray(f["L1_ffn_fc1_b"].reshape(E1 * 2 * HC, P).T),
        "brow": np.concatenate([f["L0_ffn_expert_b"].ravel(), f["L0_ffn_out_b"], f["L1_ffn_fc2_b"].ravel()]).reshape(P, -1),
        "f1": np.ascontiguousarray(f["L1_ffn_fc1_w"].transpose(0, 2, 1)),
        "f2": np.ascontiguousarray(f["L1_ffn_fc2_w"].transpose(0, 2, 1)),
    }
    nc = bacc.Bacc("TRN2", target_bir_lowering=False, num_devices=1, dynamic_dma_scratch_size=8192)
    a = {k: nc.dram_tensor(f"in_{k}", v.shape, mybir.dt.from_np(v.dtype), kind="ExternalInput").ap() for k, v in arrays.items()}
    a.update(COUNTS)
    out = nc.dram_tensor("out", [TOK + SLOTS, D], F32, kind="ExternalOutput").ap()
    build(nc, a, out)
    r = run_bass_kernel_spmd(nc, [{f"in_{k}": v for k, v in arrays.items()}], core_ids=[0])
    return r.results[0]["out"][0:TOK, :].reshape(B, N, D)


COUNTS = {"dve_turn": 98, "pool_turn": (12, 6)}
```
